# Optimizing a Trainium2 kernel written in Bass

```python
import numpy as np
import jax
import jax.numpy as jnp

def _softmax(x, axis=-1):
    return jax.nn.softmax(x, axis=axis)

def _gelu(x):
    return jax.nn.gelu(x, approximate=True)

def _silu(x):
    return jax.nn.silu(x)

def _sigmoid(x):
    return jax.nn.sigmoid(x)

def _layernorm(x, axis=-1, eps=1e-05):
    m = jnp.mean(x, axis=axis, keepdims=True)
    v = jnp.var(x, axis=axis, keepdims=True)
    return (x - m) / jnp.sqrt(v + eps)

def _scatter_add(tgt, idx, src, axis=0):
    return tgt.at[idx].add(src)

def _segment_sum(src, seg, n):
    return jax.ops.segment_sum(src, seg, n)
kernel_name = 'mk_prb_d1_jaxref_r8_5e7d71'

def setup_inputs(seed: int=0):
    np.random.seed(seed)
    _w = jnp.asarray

    def _L0_attn_setup():
        import jax, jax.numpy as jnp
        import numpy as np
        key = jax.random.key(seed)
        ks = jax.random.split(key, 5)
        B, S, D = (1, 512, 256)
        H, Dh = (16, 128)
        scale = 1.0 / np.sqrt(D).astype(np.float32)
        return {'x': jax.random.normal(ks[0], (B, S, D), dtype=jnp.float32), 'W_K': jax.random.normal(ks[1], (H, Dh, D), dtype=jnp.float32) * scale, 'W_Q': jax.random.normal(ks[2], (H, Dh, D), dtype=jnp.float32) * scale, 'W_V': jax.random.normal(ks[3], (H, Dh, D), dtype=jnp.float32) * scale, 'W_O': jax.random.normal(ks[4], (D, H * Dh), dtype=jnp.float32) * scale}
    _L0_attn_in = _L0_attn_setup()

    def _L0_ffn_setup():
        import jax, jax.numpy as jnp
        import numpy as np
        B, S, D, H = (4, 256, 256, 1024)

        def fwht(x):
            orig_shape = x.shape
            n = orig_shape[-1]
            x = x.reshape(-1, n)
            h = 1
            while h < n:
                xb = x.reshape(-1, n // (2 * h), 2, h)
                a = xb[:, :, 0, :]
                b = xb[:, :, 1, :]
                x = jnp.stack([a + b, a - b], axis=2).reshape(-1, n)
                h *= 2
            scale = jnp.asarray(1.0 / np.sqrt(n), dtype=x.dtype)
            return (x * scale).reshape(orig_shape)
        key = jax.random.key(seed)
        kx, k1, k2, k3 = jax.random.split(key, 4)
        x = jax.random.normal(kx, (B, S, D), dtype=jnp.float32)
        W1 = jax.random.normal(k1, (H, D), dtype=jnp.float32) * (1.0 / np.sqrt(D))
        W2 = jax.random.normal(k2, (D, H), dtype=jnp.float32) * (1.0 / np.sqrt(H))
        W3 = jax.random.normal(k3, (H, D), dtype=jnp.float32) * (1.0 / np.sqrt(D))
        return {'x': x, 'W1': W1, 'W2': W2, 'W3': W3}
    _L0_ffn_in = _L0_ffn_setup()
    _d = {'L0_attn_x': _L0_attn_in['x'], 'L0_attn_W_K': _L0_attn_in['W_K'], 'L0_attn_W_Q': _L0_attn_in['W_Q'], 'L0_attn_W_V': _L0_attn_in['W_V'], 'L0_attn_W_O': _L0_attn_in['W_O'], 'L0_ffn_W1': _L0_ffn_in['W1'], 'L0_ffn_W2': _L0_ffn_in['W2'], 'L0_ffn_W3': _L0_ffn_in['W3']}
    _x0 = _d['L0_attn_x']
    _d['L0_attn_x'] = jax.random.normal(jax.random.fold_in(jax.random.key(seed), 1), (1, 2048, 256), dtype=_x0.dtype)
    del _x0
    return _d

def reference(L0_attn_x, L0_attn_W_K, L0_attn_W_Q, L0_attn_W_V, L0_attn_W_O, L0_ffn_W1, L0_ffn_W2, L0_ffn_W3):

    def _L0_attn_ref(x, W_K, W_Q, W_V, W_O):
        import jax, jax.numpy as jnp
        import numpy as np
        b, pos, d_model = x.shape
        d_head = W_K.shape[1]
        k = jnp.einsum('ihd,bpd->biph', W_K, x)
        q = jnp.einsum('ihd,bpd->biph', W_Q, x)
        v = jnp.einsum('ihd,bpd->biph', W_V, x)
        scores = jnp.einsum('biph,biqh->biqp', k, q)
        mask = jnp.tril(jnp.ones((pos, pos), dtype=x.dtype))
        masked = scores * mask - jnp.float32(10000000000.0) * (1.0 - mask)
        attn = jax.nn.softmax(masked / jnp.sqrt(jnp.float32(d_head)), axis=-1)
        z = jnp.einsum('biqp,biph->biqh', attn, v)
        z_flat = jnp.transpose(z, (0, 2, 1, 3)).reshape(b, pos, -1)
        out = jnp.einsum('df,bqf->bqd', W_O, z_flat)
        return out

    def _L0_ffn_ref(x, W1, W2, W3):
        import jax, jax.numpy as jnp
        import numpy as np
        B, S, D, H = (4, 256, 256, 1024)

        def fwht(x):
            orig_shape = x.shape
            n = orig_shape[-1]
            x = x.reshape(-1, n)
            h = 1
            while h < n:
                xb = x.reshape(-1, n // (2 * h), 2, h)
                a = xb[:, :, 0, :]
                b = xb[:, :, 1, :]
                x = jnp.stack([a + b, a - b], axis=2).reshape(-1, n)
                h *= 2
            scale = jnp.asarray(1.0 / np.sqrt(n), dtype=x.dtype)
            return (x * scale).reshape(orig_shape)
        up_gate = jnp.einsum('bsd,hd->bsh', x, W1)
        up_lin = jnp.einsum('bsd,hd->bsh', x, W3)
        hidden = jax.nn.silu(up_gate) * up_lin
        hidden = fwht(hidden)
        out = jnp.einsum('bsh,dh->bsd', hidden, W2)
        return out
    x = L0_attn_x
    xn = _layernorm(x, axis=-1)
    x = x + _L0_attn_ref(xn, L0_attn_W_K, L0_attn_W_Q, L0_attn_W_V, L0_attn_W_O) + _L0_ffn_ref(xn, L0_ffn_W1, L0_ffn_W2, L0_ffn_W3)
    return x

_drawn_inputs = setup_inputs


def setup_inputs(seed=0):
    import zlib

    import numpy as np

    out = dict(_drawn_inputs(seed))
    spreads = {}
    factors = {}
    for name, (base, spread) in spreads.items():
        noise = np.random.default_rng([zlib.crc32(name.encode()), seed]).standard_normal(out[name].shape)
        drawn = base * np.exp(spread * noise) if base else spread * noise
        out[name] = jnp.asarray(drawn.astype(out[name].dtype))
    for name, factor in factors.items():
        out[name] = (out[name] * factor).astype(out[name].dtype)
    return out
```

```python
from contextlib import ExitStack

import concourse.bass as bass
from concourse import mybir

F32 = mybir.dt.float32
F32R = mybir.dt.float32r
BF16 = mybir.dt.bfloat16
ALU = mybir.AluOpType
ACT = mybir.ActivationFunctionType
AX_X = mybir.AxisListType.X

P = 128
BANK = 512
CHUNK_Q = 256
EPS = 1e-5


def attention_ffn_kernel(nc, x, w_heads, w1t, w3t, w2t, hadamard, out):
    S, D = x.shape
    HEADS = w_heads.shape[0]
    HID = w1t.shape[2]
    KD = D // P
    TILES = S // P
    QUARTERS = S // BANK
    PER_Q = BANK // P
    HT = HID // P
    CHUNKS = S // CHUNK_Q
    SCALE = float(P) ** -0.5
    HAD_SCALE = float(HID) ** -0.5
    assert D == 256 and S == 2048 and HT == 8 and KD == 2

    def banks_of(j):
        return j // PER_Q + 1

    TB = [sum(banks_of(i) for i in range(j)) for j in range(TILES + 1)]
    HEAD_BANKS = TB[TILES]

    def first_bank(j):
        if j < 4:
            return j
        return 2 * (j % 2) if j < 8 else 0

    with ExitStack() as ctx:
        def sb(name, shape, dt):
            return ctx.enter_context(nc.sbuf_tensor(name, shape, dt))

        def sem(name):
            return ctx.enter_context(nc.semaphore(name))

        ps = ctx.enter_context(nc.psum_tensor("ps", [P, 8 * BANK], F32))

        def bank(b, lo=0, hi=BANK):
            return ps[:, b * BANK + lo:b * BANK + hi]

        TRANS, Z, WOUT = 4, 6, 7

        acc = sb("acc", [P, TILES, D], F32)
        xt_hi = sb("xt_hi", [P, KD, S], F32R)
        xt_lo = sb("xt_lo", [P, KD, S], F32R)
        ident = sb("ident", [P, P], F32)
        ident_bf = sb("ident_bf", [P, P], BF16)
        ones = sb("ones", [P, 1], F32)
        mask_bf = sb("mask_bf", [P, P], BF16)

        k_hi, k_lo = sb("k_hi", [P, S], F32R), sb("k_lo", [P, S], F32R)
        q_hi, q_lo = sb("q_hi", [P, S], F32R), sb("q_lo", [P, S], F32R)
        v_hi, v_lo = sb("v_hi", [P, S], F32R), sb("v_lo", [P, S], F32R)
        pt_hi = sb("pt_hi", [P, 2 * TILES * CHUNK_Q], F32R)
        pt_lo = sb("pt_lo", [P, 2 * TILES * CHUNK_Q], F32R)
        probs = sb("probs", [P, 2, S], F32)
        z_hi, z_lo = sb("z_hi", [P, CHUNK_Q], F32R), sb("z_lo", [P, CHUNK_Q], F32R)
        w_raw = sb("w_raw", [P, 4, D], F32)
        wqkv_hi, wqkv_lo = sb("wqkv_hi", [P, 3, D], F32R), sb("wqkv_lo", [P, 3, D], F32R)
        wo_hi, wo_lo = sb("wo_hi", [P, D], F32R), sb("wo_lo", [P, D], F32R)
        bank_max = sb("bank_max", [P, TILES, 4], F32)
        neg_max = sb("neg_max", [P, TILES], F32)
        row_sum = sb("row_sum", [P, TILES], F32)
        row_rcp = sb("row_rcp", [P, TILES], F32)

        stats = sb("stats", [P, PER_Q, 6], F32)
        mean_var = sb("mean_var", [P, TILES, 2], F32)
        inv_var = sb("inv_var", [P, TILES], F32)
        rstd = sb("rstd", [P, TILES], F32)
        w2_a, w2_b = sb("w2_a", [P, HT * D], F32), sb("w2_b", [P, HT * D], F32)
        had = w2_b[:, HT * D - P:HT * D]
        xn = w_raw

        def region(t, at, n):
            return t[:, at * 2048:at * 2048 + n]

        w1_hi, w3_hi, w2_hi, hid_hi = (region(pt_hi, i, 2048) for i in range(4))
        w1_lo, w3_lo, w2_lo, hid_lo = (region(pt_lo, i, 2048) for i in range(4))
        w1_raw, w3_raw = probs[:, 0, :], probs[:, 1, :]
        gate = [probs[:, 0, i * BANK:(i + 1) * BANK] for i in range(2)]
        hidden = [probs[:, 1, i * BANK:(i + 1) * BANK] for i in range(2)]

        pt_hi4 = pt_hi[:, :].rearrange("p (b t q) -> p b t q", b=2, t=TILES)
        pt_lo4 = pt_lo[:, :].rearrange("p (b t q) -> p b t q", b=2, t=TILES)

        x_loaded = [sem(f"x_loaded{i}") for i in range(QUARTERS)]
        w1_loaded, w3_loaded = sem("w1_loaded"), sem("w3_loaded")
        w2_loaded, had_loaded = sem("w2_loaded"), sem("had_loaded")
        head_loaded = sem("head_loaded")
        out_stored = sem("out_stored")
        const_ready = sem("const_ready")
        stats_done, aggr_done, eps_done, inv_done = (
            sem("stats_done"), sem("aggr_done"), sem("eps_done"), sem("inv_done"))
        rstd_done, xn_done, xn_transposed = sem("rstd_done"), sem("xn_done"), sem("xn_transposed")
        xt_hi_done, xt_lo_done = sem("xt_hi_done"), sem("xt_lo_done")
        had_product, had_copied, w2_summed = sem("had_product"), sem("had_copied"), sem("w2_summed")
        w2_hi_done, w2_lo_done = sem("w2_hi_done"), sem("w2_lo_done")
        w13_hi_done, w13_lo_done = sem("w13_hi_done"), sem("w13_lo_done")
        gate_product, up_product = sem("gate_product"), sem("up_product")
        gate_done, hidden_done = sem("gate_done"), sem("hidden_done")
        hid_hi_done, hid_lo_done = sem("hid_hi_done"), sem("hid_lo_done")
        ffn_product, ffn_added = sem("ffn_product"), sem("ffn_added")
        wqkv_split, wo_split, pool_hi = sem("wqkv_split"), sem("wo_split"), sem("pool_hi")
        projected, proj_hi, proj_lo = sem("projected"), sem("proj_hi"), sem("proj_lo")
        scored, maxed, negmaxed, exped = sem("scored"), sem("maxed"), sem("negmaxed"), sem("exped")
        transposed, p_hi_done, p_lo_done = sem("transposed"), sem("p_hi_done"), sem("p_lo_done")
        z_product, z_hi_done, z_lo_done = sem("z_product"), sem("z_hi_done"), sem("z_lo_done")
        wo_product, rcp_done, out_added = sem("wo_product"), sem("rcp_done"), sem("out_added")

        PROJ = 3 * QUARTERS
        G_FREE = 2
        T_FREE = 2
        Z_FREE = 1
        W_FREE = 1

        block = ctx.enter_context(nc.Block())

        @block.sync
        def _(sp):
            x_v = x.rearrange("(c t p) d -> c p t d", p=P, t=PER_Q)
            out_v = out.rearrange("(c t p) d -> c p t d", p=P, t=2)
            sp.dma_start(acc[:, 0:PER_Q, :], x_v[0]).then_inc(x_loaded[0], 16)
            sp.dma_start(had, hadamard).then_inc(had_loaded, 16)
            sp.dma_start(w2_a[:, :], w2t.rearrange("p t d -> p (t d)")).then_inc(w2_loaded, 16)
            for c in range(1, QUARTERS):
                sp.dma_start(acc[:, c * PER_Q:(c + 1) * PER_Q, :], x_v[c]).then_inc(x_loaded[c], 16)
            sp.dma_start(w1_raw, w1t.rearrange("p k h -> p (k h)")).then_inc(w1_loaded, 16)
            sp.dma_start(w3_raw, w3t.rearrange("p k h -> p (k h)")).then_inc(w3_loaded, 16)
            sp.wait_ge(xn_transposed, KD * QUARTERS)
            sp.dma_start(w_raw[:, :, :], w_heads[0]).then_inc(head_loaded, 16)
            with sp.Fori(1, HEADS) as h:
                sp.wait_ge(wo_split, h)
                sp.dma_start(w_raw[:, :, :], w_heads[bass.ds(h, 1)].rearrange("a p c d -> (a p) c d")
                             ).then_inc(head_loaded, 16)
            for c in range(CHUNKS):
                sp.wait_ge(out_added, W_FREE + CHUNKS * (HEADS - 1) + c + 1)
                sp.dma_start(out_v[c], acc[:, 2 * c:2 * c + 2, :]).then_inc(out_stored, 16)
            sp.wait_ge(out_stored, 16 * CHUNKS)

        @block.gpsimd
        def _(pool):
            pool.memset(ident[:, :], 0.0).then_inc(const_ready, 1)
            pool.memset(ident_bf[:, :], 0.0).then_inc(const_ready, 1)
            pool.memset(mask_bf[:, :], 0.0).then_inc(const_ready, 1)
            pool.memset(ones[:, :], 1.0).then_inc(const_ready, 1)
            pool.wait_ge(const_ready, 4)
            for t in (ident, ident_bf):
                pool.affine_select(out=t[:, :], in_=t[:, :], compare_op=ALU.not_equal, fill=1.0, base=0,
                                   pattern=[[-1, P]], channel_multiplier=1).then_inc(const_ready, 1)
            pool.affine_select(out=mask_bf[:, :], in_=mask_bf[:, :], compare_op=ALU.is_ge,
                               fill=-1e10 * SCALE, base=0, pattern=[[-1, P]],
                               channel_multiplier=1).then_inc(const_ready, 1)

            pool.wait_ge(had_copied, 2)
            src, dst = w2_b, w2_a
            for r in range(3):
                w = D << r
                s = src[:, :].rearrange("p (g two w) -> p g two w", two=2, w=w)
                d = dst[:, :].rearrange("p (g two w) -> p g two w", two=2, w=w)
                if r:
                    pool.wait_ge(w2_summed, 2 * r)
                pool.tensor_tensor(d[:, :, 0, :], s[:, :, 0, :], s[:, :, 1, :], ALU.add).then_inc(w2_summed, 1)
                pool.tensor_tensor(d[:, :, 1, :], s[:, :, 0, :], s[:, :, 1, :], ALU.subtract
                                   ).then_inc(w2_summed, 1)
                src, dst = dst, src

            def split_qkv():
                pool.tensor_tensor(wqkv_hi[:, :, :], w_raw[:, 0:3, :], ones[:, :].to_broadcast([P, 3, D]), ALU.mult).then_inc(pool_hi, 1)

            def split_qkv_lo():
                pool.tensor_tensor(wqkv_lo[:, :, :], w_raw[:, 0:3, :], wqkv_hi[:, :, :].bitcast(F32),
                                   ALU.subtract).then_inc(wqkv_split, 1)

            def split_wo():
                pool.tensor_tensor(wo_hi[:, :], w_raw[:, 3, :], ones[:, :].to_broadcast([P, D]), ALU.mult).then_inc(pool_hi, 1)

            def split_wo_lo():
                pool.tensor_tensor(wo_lo[:, :], w_raw[:, 3, :], wo_hi[:, :].bitcast(F32),
                                   ALU.subtract).then_inc(wo_split, 1)

            pool.wait_ge(head_loaded, 16)
            split_qkv()
            pool.wait_ge(pool_hi, 1)
            split_qkv_lo()
            split_wo()
            pool.wait_ge(pool_hi, 2)
            split_wo_lo()
            with pool.Fori(1, HEADS) as h:
                pool.wait_ge(head_loaded, 16 * h + 16)
                pool.wait_ge(projected, PROJ * h)
                split_qkv()
                pool.wait_ge(pool_hi, 2 * h + 1)
                split_qkv_lo()
                pool.wait_ge(wo_product, CHUNKS * h)
                split_wo()
                pool.wait_ge(pool_hi, 2 * h + 2)
                split_wo_lo()

        @block.scalar
        def _(act):
            for i in range(2):
                act.wait_ge(had_product, 2 * i + 2)
                act.activation(w2_b[:, i * 1024:(i + 1) * 1024], ps[:, i * 1024:(i + 1) * 1024], ACT.Copy,
                               scale=HAD_SCALE).then_inc(had_copied, 1)

            for c in range(QUARTERS):
                act.wait_ge(inv_done, c + 1)
                act.activation(rstd[:, c * PER_Q:(c + 1) * PER_Q], inv_var[:, c * PER_Q:(c + 1) * PER_Q],
                               ACT.Sqrt).then_inc(rstd_done, 1)
            for c in range(QUARTERS):
                for k in range(KD):
                    act.wait_ge(xn_transposed, KD * c + k + 1)
                    act.copy(xt_hi[:, k, c * BANK:(c + 1) * BANK], bank(TRANS + 2 * (c % 2) + k)
                             ).then_inc(xt_hi_done, 1)
            act.wait_ge(w1_loaded, 16)
            act.copy(w1_hi, w1_raw).then_inc(w13_hi_done, 1)
            act.wait_ge(w3_loaded, 16)
            act.copy(w3_hi, w3_raw).then_inc(w13_hi_done, 1)
            act.wait_ge(w13_lo_done, 2)
            act.wait_ge(w2_summed, 6)
            act.copy(w2_hi, w2_a[:, :]).then_inc(w2_hi_done, 1)

            def hidden_to_hi(c, t):
                act.wait_ge(hidden_done, HT * c + t + 1 + G_FREE)
                act.copy(hid_hi[:, (t % 4) * BANK:(t % 4 + 1) * BANK], hidden[t % 2]).then_inc(hid_hi_done, 1)

            with act.Fori(0, QUARTERS) as c:
                for t in range(HT):
                    act.wait_ge(gate_product, HT * c + t + 1)
                    act.activation(gate[t % 2], bank(2 * (t % 2)), ACT.Silu).then_inc(gate_done, 1)
                    if t >= 1:
                        hidden_to_hi(c, t - 1)
                hidden_to_hi(c, HT - 1)

            def project(hh, first, last):
                for i in range(first, last):
                    which, b = i // QUARTERS, i % QUARTERS
                    dst = (k_hi, q_hi, v_hi)[which]
                    act.wait_ge(projected, PROJ * hh + i + 1)
                    act.activation(dst[:, b * BANK:(b + 1) * BANK], bank(b), ACT.Copy,
                                   scale=SCALE if which == 1 else 1.0).then_inc(proj_hi, 1)

            def head(h, last):
                def p_to_hi(j, g):
                    n = min(4, j + 1 - 4 * g)
                    at = TB[j] + g
                    act.wait_ge(transposed, HEAD_BANKS * h + at + 1)
                    act.copy(pt_hi4[:, (j // 2) % 2, 4 * g:4 * g + n, (j % 2) * P:(j % 2 + 1) * P],
                             bank(TRANS + at % 2, 0, n * P).rearrange("p (t q) -> p t q", q=P)
                             ).then_inc(p_hi_done, 1)

                def z_to_hi(c):
                    act.wait_ge(z_product, CHUNKS * h + c + 1)
                    act.copy(z_hi[:, :], bank(Z, 0, CHUNK_Q)).then_inc(z_hi_done, 1)

                for s in range(TILES + 1):
                    if s >= 5 and s % 2:
                        z_to_hi((s - 5) // 2)
                    nt = banks_of(s - 1) if s else 0
                    if s == TILES and not last:
                        project(h + 1, 0, 2 * QUARTERS)
                    for g in range(min(nt, 3)):
                        p_to_hi(s - 1, g)
                    if s < TILES:
                        L, b0 = (s + 1) * P, first_bank(s)
                        act.wait_ge(negmaxed, TILES * h + s + 1)
                        act.activation(probs[:, s % 2, 0:L], ps[:, b0 * BANK:b0 * BANK + L], ACT.Exp,
                                       bias=neg_max[:, s:s + 1], accum_out=row_sum[:, s:s + 1]
                                       ).then_inc(exped, 1)
                    for g in range(3, nt):
                        p_to_hi(s - 1, g)
                z_to_hi(CHUNKS - 2)
                if last:
                    z_to_hi(CHUNKS - 1)
                else:
                    z_to_hi(CHUNKS - 1)
                    project(h + 1, 2 * QUARTERS, PROJ)

            project(0, 0, PROJ)
            with act.Fori(0, HEADS - 1) as h:
                head(h, False)
            head(HEADS - 1, True)

        @block.vector
        def _(dve):
            def normalize(c):
                dve.wait_ge(rstd_done, c + 1)
                if c:
                    dve.wait_ge(xn_transposed, KD * c)
                for t in range(PER_Q):
                    i = c * PER_Q + t
                    dve.tensor_scalar(xn[:, t, :], acc[:, i, :], mean_var[:, i, 0:1], rstd[:, i:i + 1],
                                      ALU.subtract, ALU.mult).then_inc(xn_done, 1)

            def xt_to_lo(c):
                for k in range(KD):
                    dve.wait_ge(xt_hi_done, KD * c + k + 1)
                    sl = slice(c * BANK, (c + 1) * BANK)
                    dve.tensor_tensor(xt_lo[:, k, sl], bank(TRANS + 2 * (c % 2) + k),
                                      xt_hi[:, k, sl].bitcast(F32), ALU.subtract).then_inc(xt_lo_done, 1)

            for c in range(QUARTERS):
                q = slice(c * PER_Q, (c + 1) * PER_Q)
                dve.wait_ge(x_loaded[c], 16)
                for t in range(PER_Q):
                    dve.bn_stats(stats[:, t, :], acc[:, c * PER_Q + t, :]).then_inc(stats_done, 1)
                dve.wait_ge(stats_done, PER_Q * (c + 1))
                for t in range(PER_Q):
                    dve.bn_aggr(mean_var[:, c * PER_Q + t, :], stats[:, t, :]).then_inc(aggr_done, 1)
                dve.wait_ge(aggr_done, PER_Q * (c + 1))
                dve.tensor_scalar(inv_var[:, q], mean_var[:, q, 1], EPS, None, ALU.add).then_inc(eps_done, 1)
                dve.wait_ge(eps_done, c + 1)
                dve.reciprocal(inv_var[:, q], inv_var[:, q]).then_inc(inv_done, 1)
            for c in range(QUARTERS):
                normalize(c)
                if c:
                    xt_to_lo(c - 1)
            dve.wait_ge(w13_hi_done, 1)
            dve.tensor_tensor(w1_lo, w1_raw, w1_hi.bitcast(F32), ALU.subtract).then_inc(w13_lo_done, 1)
            xt_to_lo(QUARTERS - 1)
            dve.wait_ge(w13_hi_done, 2)
            dve.tensor_tensor(w3_lo, w3_raw, w3_hi.bitcast(F32), ALU.subtract).then_inc(w13_lo_done, 1)
            dve.wait_ge(had_copied, 2)
            dve.memset(bank_max[:, 1, :], 0.0).then_inc(hidden_done, G_FREE)
            dve.memset(bank_max[:, 2, :], 0.0).then_inc(hid_lo_done, G_FREE)
            dve.memset(bank_max[:, 0, :], 0.0).then_inc(ffn_added, 1)
            dve.wait_ge(w2_hi_done, 1)
            dve.tensor_tensor(w2_lo, w2_a[:, :], w2_hi.bitcast(F32), ALU.subtract).then_inc(w2_lo_done, 1)

            def hidden_to_lo(c, t):
                sl = slice((t % 4) * BANK, (t % 4 + 1) * BANK)
                dve.wait_ge(hid_hi_done, HT * c + t + 1)
                dve.tensor_tensor(hid_lo[:, sl], hidden[t % 2], hid_hi[:, sl].bitcast(F32),
                                  ALU.subtract).then_inc(hid_lo_done, 1)

            with dve.Fori(0, QUARTERS) as c:
                for t in range(HT):
                    dve.wait_ge(up_product, HT * c + t + 1)
                    dve.wait_ge(gate_done, HT * c + t + 1)
                    dve.wait_ge(hid_lo_done, HT * c + t - 1 + G_FREE)
                    dve.tensor_tensor(hidden[t % 2], gate[t % 2], bank(2 * (t % 2) + 1), ALU.mult
                                      ).then_inc(hidden_done, 1)
                    if t >= 1:
                        hidden_to_lo(c, t - 1)
                hidden_to_lo(c, HT - 1)
                for t in range(PER_Q):
                    a = acc[:, bass.ds(c * PER_Q + t, 1), :].rearrange("p a d -> p (a d)")
                    dve.wait_ge(ffn_product, PER_Q * c + t + 1)
                    dve.tensor_tensor(a, bank(TRANS + t, 0, D), a, ALU.add).then_inc(ffn_added, 1)

            dve.wait_ge(ffn_added, PER_Q * QUARTERS + 1)
            dve.memset(bank_max[:, 0, :], 0.0).then_inc(p_lo_done, T_FREE)
            dve.memset(bank_max[:, 1, :], 0.0).then_inc(z_lo_done, Z_FREE)
            dve.memset(bank_max[:, 2, :], 0.0).then_inc(out_added, W_FREE)

            def project(hh, first, last):
                for i in range(first, last):
                    which, b = i // QUARTERS, i % QUARTERS
                    hi, lo = ((k_hi, k_lo), (q_hi, q_lo), (v_hi, v_lo))[which]
                    sl = slice(b * BANK, (b + 1) * BANK)
                    dve.wait_ge(proj_hi, PROJ * hh + i + 1)
                    if which == 1:
                        dve.scalar_tensor_tensor(out=lo[:, sl], in0=bank(b), scalar=SCALE,
                                                 in1=hi[:, sl].bitcast(F32), op0=ALU.mult,
                                                 op1=ALU.subtract).then_inc(proj_lo, 1)
                    else:
                        dve.tensor_tensor(lo[:, sl], bank(b), hi[:, sl].bitcast(F32),
                                          ALU.subtract).then_inc(proj_lo, 1)

            def head(h, last):
                def bank_maximum(j, b):
                    n = min(BANK, (j + 1) * P - b * BANK)
                    dve.wait_ge(scored, HEAD_BANKS * h + TB[j] + b + 1)
                    one = banks_of(j) == 1
                    dst = neg_max[:, j:j + 1] if one else bank_max[:, j, b:b + 1]
                    dve.tensor_reduce(dst, bank(first_bank(j) + b, 0, n), AX_X, ALU.max,
                                      negate=one).then_inc(negmaxed if one else maxed, 1)

                def negated_maximum(j):
                    if banks_of(j) > 1:
                        dve.wait_ge(maxed, (HEAD_BANKS - 4) * h + TB[j + 1] - 4)
                        dve.tensor_reduce(neg_max[:, j:j + 1], bank_max[:, j, 0:banks_of(j)], AX_X, ALU.max,
                                          negate=True).then_inc(negmaxed, 1)

                def p_to_lo(j, g):
                    n = min(4, j + 1 - 4 * g)
                    at = TB[j] + g
                    dve.wait_ge(p_hi_done, HEAD_BANKS * h + at + 1)
                    where = (slice(None), (j // 2) % 2, slice(4 * g, 4 * g + n), slice((j % 2) * P, (j % 2 + 1) * P))
                    dve.tensor_tensor(pt_lo4[where], bank(TRANS + at % 2, 0, n * P).rearrange("p (t q) -> p t q", q=P),
                                      pt_hi4[where].bitcast(F32), ALU.subtract).then_inc(p_lo_done, 1)

                def z_to_lo(c):
                    dve.wait_ge(z_hi_done, CHUNKS * h + c + 1)
                    dve.tensor_tensor(z_lo[:, :], bank(Z, 0, CHUNK_Q), z_hi[:, :].bitcast(F32),
                                      ALU.subtract).then_inc(z_lo_done, 1)

                def reciprocals(c):
                    dve.wait_ge(exped, TILES * h + 2 * c + 2)
                    dve.reciprocal(row_rcp[:, 2 * c:2 * c + 2], row_sum[:, 2 * c:2 * c + 2]).then_inc(rcp_done, 1)

                def add_output(c):
                    dve.wait_ge(rcp_done, CHUNKS * h + c + 1)
                    dve.wait_ge(wo_product, CHUNKS * h + c + 1)
                    for t in range(2):
                        j = 2 * c + t
                        ins = dve.scalar_tensor_tensor(out=acc[:, j, :], in0=bank(WOUT, t * D, (t + 1) * D),
                                                       scalar=row_rcp[:, j:j + 1], in1=acc[:, j, :],
                                                       op0=ALU.mult, op1=ALU.add)
                    ins.then_inc(out_added, 1)

                for s in range(TILES + 1):
                    nt = banks_of(s - 1) if s else 0
                    nb = banks_of(s) if s < TILES else 0
                    c = (s - 5) // 2 if s >= 5 and s % 2 else None
                    if s == TILES and not last:
                        project(h + 1, 0, 2 * QUARTERS)
                    if nb:
                        bank_maximum(s, 0)
                    if c is not None:
                        z_to_lo(c)
                        reciprocals(c)
                    if nb > 1:
                        bank_maximum(s, 1)
                        p_to_lo(s - 1, 0)
                        for b in range(2, nb):
                            bank_maximum(s, b)
                    negated_maximum(s) if nb else None
                    for g in range(1 if nb > 1 else 0, nt):
                        p_to_lo(s - 1, g)
                    if c is not None:
                        add_output(c)
                z_to_lo(CHUNKS - 2)
                reciprocals(CHUNKS - 2)
                add_output(CHUNKS - 2)
                reciprocals(CHUNKS - 1)
                z_to_lo(CHUNKS - 1)
                if not last:
                    project(h + 1, 2 * QUARTERS, PROJ)
                add_output(CHUNKS - 1)

            project(0, 0, PROJ)
            with dve.Fori(0, HEADS - 1) as h:
                head(h, False)
            head(HEADS - 1, True)

        @block.tensor
        def _(pe):
            def mm3(dst, a, b, start, stop):
                pe.matmul(dst, a[0], b[0], start=start, stop=False, skip_group_check=True)
                pe.matmul(dst, a[0], b[1], start=False, stop=False, skip_group_check=True)
                return pe.matmul(dst, a[1], b[0], start=False, stop=stop, skip_group_check=True)

            pe.wait_ge(had_loaded, 16)
            pe.wait_ge(w2_loaded, 16)
            for i in range(4):
                pe.matmul(bank(i), had, w2_a[:, i * BANK:(i + 1) * BANK], start=True, stop=True
                          ).then_inc(had_product, 1)

            pe.wait_ge(const_ready, 7)
            for c in range(QUARTERS):
                pe.wait_ge(xn_done, PER_Q * (c + 1))
                if c >= 2:
                    pe.wait_ge(xt_lo_done, KD * (c - 1))
                for k in range(KD):
                    for t in range(PER_Q):
                        ins = pe.transpose(bank(TRANS + 2 * (c % 2) + k, t * P, (t + 1) * P),
                                           xn[:, t, k * P:(k + 1) * P], ident[:, :])
                    ins.then_inc(xn_transposed, 1)

            pe.wait_ge(xt_lo_done, KD * QUARTERS)
            pe.wait_ge(w13_lo_done, 2)
            pe.wait_ge(w2_lo_done, 1)

            def down(c, t):
                pe.wait_ge(hid_lo_done, HT * c + t + 1 + G_FREE)
                if t == 0:
                    pe.wait_ge(ffn_added, PER_Q * c + 1)
                for q in range(PER_Q):
                    sl = slice((t % 4) * BANK + q * P, (t % 4) * BANK + (q + 1) * P)
                    ins = mm3(bank(TRANS + q, 0, D), (hid_hi[:, sl], hid_lo[:, sl]),
                              (w2_hi[:, t * D:(t + 1) * D], w2_lo[:, t * D:(t + 1) * D]), t == 0, t == HT - 1)
                    if t == HT - 1:
                        ins.then_inc(ffn_product, 1)

            with pe.Fori(0, QUARTERS) as c:
                for t in range(HT):
                    pe.wait_ge(hidden_done, HT * c + t - 1 + G_FREE)
                    for b, hi, lo, done in ((0, w1_hi, w1_lo, gate_product), (1, w3_hi, w3_lo, up_product)):
                        for k in range(KD):
                            sl = slice(k * HID + t * P, k * HID + (t + 1) * P)
                            xs = (xt_hi[:, k, bass.ds(c * BANK, BANK)], xt_lo[:, k, bass.ds(c * BANK, BANK)])
                            ins = mm3(bank(2 * (t % 2) + b), (hi[:, sl], lo[:, sl]), xs, k == 0, k == KD - 1)
                        ins.then_inc(done, 1)
                    if t >= 2:
                        down(c, t - 2)
                down(c, HT - 2)
                down(c, HT - 1)

            def project(hh, first, last):
                for i in range(first, last):
                    which, b = i // QUARTERS, i % QUARTERS
                    if i >= QUARTERS:
                        pe.wait_ge(proj_lo, PROJ * hh + i - QUARTERS + 1)
                    sl = slice(b * BANK, (b + 1) * BANK)
                    if which < 2:
                        w = 1 - which
                        for k in range(KD):
                            ws = slice(k * P, (k + 1) * P)
                            ins = mm3(bank(b), (wqkv_hi[:, w, ws], wqkv_lo[:, w, ws]),
                                      (xt_hi[:, k, sl], xt_lo[:, k, sl]), k == 0, k == KD - 1)
                    else:
                        for t in range(PER_Q):
                            ts = slice(b * BANK + t * P, b * BANK + (t + 1) * P)
                            for k in range(KD):
                                ws = slice(k * P, (k + 1) * P)
                                ins = mm3(bank(b, t * P, (t + 1) * P), (xt_hi[:, k, ts], xt_lo[:, k, ts]),
                                          (wqkv_hi[:, 2, ws], wqkv_lo[:, 2, ws]), k == 0, k == KD - 1)
                    ins.then_inc(projected, 1)

            def head(h, last):
                def scores(j, b):
                    if b == 0:
                        if j < 4:
                            pe.wait_ge(proj_lo, PROJ * h + 2 * QUARTERS + j + 1)
                        else:
                            pe.wait_ge(exped, TILES * h + (j - 1 if j < 8 else j))
                    n = min(BANK, (j + 1) * P - b * BANK)
                    qs, ks = slice(j * P, (j + 1) * P), slice(b * BANK, b * BANK + n)
                    dst = bank(first_bank(j) + b, 0, n)
                    diagonal = b == banks_of(j) - 1
                    ins = mm3(dst, (q_hi[:, qs], q_lo[:, qs]), (k_hi[:, ks], k_lo[:, ks]), True, not diagonal)
                    if diagonal:
                        ins = pe.matmul(bank(first_bank(j) + b, n - P, n), ident_bf[:, :], mask_bf[:, :],
                                        start=False, stop=True, skip_group_check=True)
                    ins.then_inc(scored, 1)

                def transposes(j, g):
                    at = TB[j] + g
                    if g == 0:
                        pe.wait_ge(exped, TILES * h + j + 1)
                    pe.wait_ge(p_lo_done, HEAD_BANKS * h + at - 1 + T_FREE)
                    for i in range(4 * g, min(4 * g + 4, j + 1)):
                        ins = pe.transpose(bank(TRANS + at % 2, (i % 4) * P, (i % 4 + 1) * P),
                                           probs[:, j % 2, i * P:(i + 1) * P], ident[:, :])
                    ins.then_inc(transposed, 1)

                def weighted_sum(c, first, last):
                    if first == 0:
                        pe.wait_ge(z_lo_done, CHUNKS * h + c + Z_FREE)
                    for i in range(first, last):
                        if i % 4 == 0 or i == first:
                            pe.wait_ge(p_lo_done, HEAD_BANKS * h + TB[2 * c + 1] + i // 4 + 1 + T_FREE)
                        lo = P if i == 2 * c + 1 else 0
                        ks = slice(i * P, (i + 1) * P)
                        ins = mm3(bank(Z, lo, CHUNK_Q), (v_hi[:, ks], v_lo[:, ks]),
                                  (pt_hi4[:, c % 2, i, lo:CHUNK_Q], pt_lo4[:, c % 2, i, lo:CHUNK_Q]),
                                  i == 0, i == 2 * c + 1)
                    if last == 2 * c + 2:
                        ins.then_inc(z_product, 1)

                def output(c):
                    pe.wait_ge(z_lo_done, CHUNKS * h + c + 1 + Z_FREE)
                    pe.wait_ge(out_added, CHUNKS * h + c + W_FREE)
                    if c == 0:
                        pe.wait_ge(wo_split, h + 1)
                    for t in range(2):
                        qs = slice(t * P, (t + 1) * P)
                        ins = mm3(bank(WOUT, t * D, (t + 1) * D), (z_hi[:, qs], z_lo[:, qs]),
                                  (wo_hi[:, :], wo_lo[:, :]), True, True)
                    ins.then_inc(wo_product, 1)

                for s in range(TILES + 1):
                    nt = banks_of(s - 1) if s else 0
                    nb = banks_of(s) if s < TILES else 0
                    if s == TILES and not last:
                        pe.wait_ge(wqkv_split, h + 2)
                        pe.wait_ge(exped, TILES * h + TILES)
                        project(h + 1, 0, 2 * QUARTERS)
                    for b in range(nb):
                        scores(s, b)
                        if b < min(2, nt):
                            transposes(s - 1, b)
                    rest = list(range(min(2, nt, nb), nt))
                    if rest:
                        transposes(s - 1, rest.pop(0))
                    if s >= 5 and s % 2:
                        output((s - 5) // 2)
                    part = []
                    if s >= 3 and s % 2:
                        c = (s - 3) // 2
                        part = [(c, 0, (c + 1) // 2), (c, (c + 1) // 2, c + 1)]
                    elif s >= 4:
                        c = (s - 4) // 2
                        part = [(c, c + 1, c + 1 + (c + 1) // 2), (c, c + 1 + (c + 1) // 2, 2 * c + 2)]
                    for n, (c, a, b) in enumerate(part):
                        if a < b:
                            weighted_sum(c, a, b)
                        if rest:
                            transposes(s - 1, rest.pop(0))
                    while rest:
                        transposes(s - 1, rest.pop(0))
                c = CHUNKS - 1
                weighted_sum(c, 0, c + 1)
                output(c - 1)
                weighted_sum(c, c + 1, 2 * c + 2)
                if not last:
                    project(h + 1, 2 * QUARTERS, PROJ)
                output(c)

            pe.wait_ge(wqkv_split, 1)
            pe.wait_ge(hidden_done, HT * QUARTERS + G_FREE)
            project(0, 0, PROJ)
            with pe.Fori(0, HEADS - 1) as h:
                head(h, False)
            head(HEADS - 1, True)


def kernel(L0_attn_x, L0_attn_W_K, L0_attn_W_Q, L0_attn_W_V, L0_attn_W_O, L0_ffn_W1, L0_ffn_W2, L0_ffn_W3):
    import numpy as np
    import concourse.bacc as bacc
    from concourse.bass_utils import run_bass_kernel_spmd

    x = np.ascontiguousarray(L0_attn_x)[0]
    heads, dh, d = L0_attn_W_Q.shape
    hid = L0_ffn_W1.shape[0]

    def by_model(w):
        return np.asarray(w).T.reshape(d // P, P, -1).transpose(1, 0, 2)

    def head_weights(w):
        return np.asarray(w).transpose(0, 2, 1).reshape(heads, d // P, P, dh).transpose(0, 2, 1, 3).reshape(
            heads, P, -1)

    w_o = np.asarray(L0_attn_W_O).T.reshape(heads, dh, d)
    h128 = np.array([[1 - 2 * (bin(i & j).count("1") & 1) for j in range(P)] for i in range(P)], np.float32)
    arrays = {
        "x": x,
        "w_heads": np.ascontiguousarray(np.stack(
            [head_weights(L0_attn_W_Q), head_weights(L0_attn_W_K), head_weights(L0_attn_W_V), w_o], axis=2)),
        "w1t": np.ascontiguousarray(by_model(L0_ffn_W1)),
        "w3t": np.ascontiguousarray(by_model(L0_ffn_W3)),
        "w2t": np.ascontiguousarray(np.asarray(L0_ffn_W2).T.reshape(hid // P, P, d).transpose(1, 0, 2)),
        "hadamard": h128,
    }
    nc = bacc.Bacc("TRN2", target_bir_lowering=False, num_devices=1)
    args = [nc.dram_tensor(n, a.shape, mybir.dt.from_np(a.dtype), kind="ExternalInput").ap()
            for n, a in arrays.items()]
    out = nc.dram_tensor("out", x.shape, F32, kind="ExternalOutput").ap()
    attention_ffn_kernel(nc, *args, out)
    r = run_bass_kernel_spmd(nc, [arrays], core_ids=[0])
    return r.results[0]["out"].reshape(L0_attn_x.shape)
```

```python
from contextlib import ExitStack

import concourse.bass as bass
from concourse import mybir

F32 = mybir.dt.float32
F32R = mybir.dt.float32r
BF16 = mybir.dt.bfloat16
ALU = mybir.AluOpType
ACT = mybir.ActivationFunctionType
AX_X = mybir.AxisListType.X

P = 128
BANK = 512
CHUNK_Q = 256
EPS = 1e-5


def attention_ffn_kernel(nc, x, w_heads, w1t, w3t, w2t, hadamard, out):
    S, D = x.shape
    HEADS = w_heads.shape[0]
    HID = w1t.shape[2]
    KD = D // P
    TILES = S // P
    QUARTERS = S // BANK
    PER_Q = BANK // P
    HT = HID // P
    CHUNKS = S // CHUNK_Q
    SCALE = float(P) ** -0.5
    HAD_SCALE = float(HID) ** -0.5
    assert D == 256 and S == 2048 and HT == 8 and KD == 2

    def banks_of(j):
        return j // PER_Q + 1

    SCORE_BANKS = 4
    ORDERS = ["s"] + ["st"] * 3 + ["sst"] + ["sstt"] * 3 + ["stsst"] + ["stsstt"] * 3 + ["stsstst"] + ["stsstst"] * 3

    def score_bank(j, b):
        return (TB[j] + b) % SCORE_BANKS

    def exps_of(j):
        n = banks_of(j)
        if n <= 2:
            return [(0, n)]
        cut = 1 if score_bank(j, 1) == 0 else 2 if score_bank(j, 2) == 0 else 1 if j in (8, 11, 12, 14) else 2
        return [(0, cut), (cut, n)]

    TB = [sum(banks_of(i) for i in range(j)) for j in range(TILES + 1)]
    HEAD_BANKS = TB[TILES]
    assert HEAD_BANKS % SCORE_BANKS == 0

    def exp_of(j, b):
        return EX[j] + [lo <= b < hi for lo, hi in exps_of(j)].index(True)

    def v_items(s):
        return ([("V", s)] if s < QUARTERS else []) + ([("VT", s - 1)] if 1 <= s <= QUARTERS else [])

    EX = [sum(len(exps_of(i)) for i in range(j)) for j in range(TILES + 1)]

    BANK_OF = [(j, b) for j in range(TILES) for b in range(banks_of(j))]

    RING = 3
    ITEMS = []
    for slot in range(TILES):
        nt = banks_of(slot - 1) if slot else 0
        ITEMS += [(slot - 1, g) for g in range(min(nt, 3))] + v_items(slot)
        ITEMS += [(slot - 1, 3)] if nt == 4 else []
        ITEMS += [("O", (slot - 5) // 2)] if slot >= 5 and slot % 2 else []
    ITEMS += [(TILES - 1, 0), (TILES - 1, 1), ("O", CHUNKS - 2), (TILES - 1, 2), (TILES - 1, 3),
              ("O", CHUNKS - 1), None]
    ITEM = {item: n for n, item in enumerate(ITEMS)}
    SPLIT_ITEMS = [item for item in ITEMS if item and item[0] not in ("V", "O")]
    FREED_ITEMS = [item for item in ITEMS if item and item[0] != "O"]
    assert len(ITEMS) % RING == 0

    with ExitStack() as ctx:
        def sb(name, shape, dt):
            return ctx.enter_context(nc.sbuf_tensor(name, shape, dt))

        def sem(name):
            return ctx.enter_context(nc.semaphore(name))

        ps = ctx.enter_context(nc.psum_tensor("ps", [P, 8 * BANK], F32))

        def bank(b, lo=0, hi=BANK):
            return ps[:, b * BANK + lo:b * BANK + hi]

        TRANS, Z = 4, 7

        acc = sb("acc", [P, TILES, D], F32)
        xt_hi = sb("xt_hi", [P, KD, S], F32R)
        xt_lo = sb("xt_lo", [P, KD, S], F32R)
        ident = sb("ident", [P, P], F32)
        ident_bf = sb("ident_bf", [P, P], BF16)
        ones = sb("ones", [P, 1], F32)
        mask_bf = sb("mask_bf", [P, P], BF16)
        table_use = sb("table_use", [P, 2], F32)

        k_hi, k_lo = sb("k_hi", [P, S], F32R), sb("k_lo", [P, S], F32R)
        q_hi, q_lo = sb("q_hi", [P, S], F32R), sb("q_lo", [P, S], F32R)
        v_hi, v_lo = sb("v_hi", [P, S], F32R), sb("v_lo", [P, S], F32R)
        pt_hi = sb("pt_hi", [P, 2 * TILES * CHUNK_Q], F32R)
        pt_lo = sb("pt_lo", [P, 2 * TILES * CHUNK_Q], F32R)
        probs = sb("probs", [P, 2, S], F32)
        z_hi, z_lo = sb("z_hi", [P, CHUNK_Q], F32R), sb("z_lo", [P, CHUNK_Q], F32R)
        w_raw = sb("w_raw", [P, 4, D], F32)
        wqkv_hi, wqkv_lo = sb("wqkv_hi", [P, 3, D], F32R), sb("wqkv_lo", [P, 3, D], F32R)
        wo_hi, wo_lo = sb("wo_hi", [P, D], F32R), sb("wo_lo", [P, D], F32R)
        bank_max = sb("bank_max", [P, TILES, 4], F32)
        neg_max = sb("neg_max", [P, TILES], F32)

        stats = sb("stats", [P, PER_Q, 6], F32)
        mean_var = sb("mean_var", [P, TILES, 2], F32)
        inv_var = sb("inv_var", [P, TILES], F32)
        rstd = sb("rstd", [P, TILES], F32)
        w2_a, w2_b = sb("w2_a", [P, HT * D], F32), sb("w2_b", [P, HT * D], F32)
        had = w2_b[:, HT * D - P:HT * D]
        share = w2_a[:, 0:4 * D].rearrange("p (b t d) -> p b t d", b=2, t=2)
        row_part = w2_b[:, 0:2 * TILES].rearrange("p (t e) -> p t e", e=2)
        v_raw = [w2_b[:, (1 + i) * BANK:(2 + i) * BANK] for i in range(2)]
        row_sum, row_rcp = w2_b[:, 2 * TILES:3 * TILES], w2_b[:, 3 * TILES:4 * TILES]
        xn = w_raw

        def region(t, at, n):
            return t[:, at * 2048:at * 2048 + n]

        w1_hi, w3_hi, w2_hi, hid_hi = (region(pt_hi, i, 2048) for i in range(4))
        w1_lo, w3_lo, w2_lo, hid_lo = (region(pt_lo, i, 2048) for i in range(4))
        w1_raw, w3_raw = probs[:, 0, :], probs[:, 1, :]
        gate = [probs[:, 0, i * BANK:(i + 1) * BANK] for i in range(2)]
        hidden = [probs[:, 1, i * BANK:(i + 1) * BANK] for i in range(2)]

        pt_hi4 = pt_hi[:, :].rearrange("p (b t q) -> p b t q", b=2, t=TILES)
        pt_lo4 = pt_lo[:, :].rearrange("p (b t q) -> p b t q", b=2, t=TILES)

        x_loaded = [sem(f"x_loaded{i}") for i in range(QUARTERS)]
        w1_loaded, w3_loaded = sem("w1_loaded"), sem("w3_loaded")
        w2_loaded, had_loaded = sem("w2_loaded"), sem("had_loaded")
        head_loaded = sem("head_loaded")
        out_stored = sem("out_stored")
        const_ready = sem("const_ready")
        stats_done, aggr_done, eps_done, inv_done = (
            sem("stats_done"), sem("aggr_done"), sem("eps_done"), sem("inv_done"))
        rstd_done, xn_done, xn_transposed = sem("rstd_done"), sem("xn_done"), sem("xn_transposed")
        xt_hi_done, xt_lo_done = sem("xt_hi_done"), sem("xt_lo_done")
        had_product, had_copied, w2_summed = sem("had_product"), sem("had_copied"), sem("w2_summed")
        w2_hi_done, w2_lo_done = sem("w2_hi_done"), sem("w2_lo_done")
        w13_hi_done, w13_lo_done = sem("w13_hi_done"), sem("w13_lo_done")
        gate_product, up_product = sem("gate_product"), sem("up_product")
        gate_done, hidden_done = sem("gate_done"), sem("hidden_done")
        hid_hi_done, hid_lo_done = sem("hid_hi_done"), sem("hid_lo_done")
        ffn_product, ffn_added = sem("ffn_product"), sem("ffn_added")
        wqkv_split, wo_split, pool_hi = sem("wqkv_split"), sem("wo_split"), sem("pool_hi")
        projected, proj_hi, proj_lo = sem("projected"), sem("proj_hi"), sem("proj_lo")
        scored, maxed, negmaxed, exped = sem("scored"), sem("maxed"), sem("negmaxed"), sem("exped")
        ring_filled, ring_hi, ring_freed = sem("ring_filled"), sem("ring_hi"), sem("ring_freed")
        z_product, z_hi_done, z_lo_done = sem("z_product"), sem("z_hi_done"), sem("z_lo_done")
        wo_product, rcp_done, summed = sem("wo_product"), sem("rcp_done"), sem("summed")
        shared, out_added = sem("shared"), sem("out_added")

        PROJ = 2 * QUARTERS
        G_FREE = 2
        R_FREE = RING
        Z_FREE = 1
        O_FREE = 1
        SHARE_FREE = 2

        def ring_bank(item):
            return TRANS + ITEM[item] % RING

        def filled(h, item):
            return len(FREED_ITEMS) * h + FREED_ITEMS.index(item) + 1

        def split_hi(h, item):
            return len(SPLIT_ITEMS) * h + SPLIT_ITEMS.index(item) + 1

        def freed(h, item):
            return len(FREED_ITEMS) * h + FREED_ITEMS.index(item) + 1 + R_FREE

        block = ctx.enter_context(nc.Block())

        @block.sync
        def _(sp):
            x_v = x.rearrange("(c t p) d -> c p t d", p=P, t=PER_Q)
            out_v = out.rearrange("(c t p) d -> c p t d", p=P, t=2)
            sp.dma_start(had, hadamard).then_inc(had_loaded, 16)
            sp.dma_start(w2_a[:, :], w2t.rearrange("p t d -> p (t d)")).then_inc(w2_loaded, 16)
            for c in range(QUARTERS):
                sp.dma_start(acc[:, c * PER_Q:(c + 1) * PER_Q, :], x_v[c]).then_inc(x_loaded[c], 16)
            sp.dma_start(w1_raw, w1t.rearrange("p k h -> p (k h)")).then_inc(w1_loaded, 16)
            sp.dma_start(w3_raw, w3t.rearrange("p k h -> p (k h)")).then_inc(w3_loaded, 16)
            sp.wait_ge(xn_transposed, TILES // 2)
            sp.dma_start(w_raw[:, :, :], w_heads[0]).then_inc(head_loaded, 16)
            with sp.Fori(1, HEADS) as h:
                sp.wait_ge(wo_split, h)
                sp.dma_start(w_raw[:, :, :], w_heads[bass.ds(h, 1)].rearrange("a p c d -> (a p) c d")
                             ).then_inc(head_loaded, 16)
            for c in range(CHUNKS):
                sp.wait_ge(out_added, SHARE_FREE + CHUNKS * (HEADS - 1) + c + 1)
                sp.dma_start(out_v[c], acc[:, 2 * c:2 * c + 2, :]).then_inc(out_stored, 16)
            sp.wait_ge(out_stored, 16 * CHUNKS)

        @block.gpsimd
        def _(pool):
            pool.memset(ident[:, :], 0.0).then_inc(const_ready, 1)
            pool.memset(ident_bf[:, :], 0.0).then_inc(const_ready, 1)
            pool.memset(mask_bf[:, :], 0.0).then_inc(const_ready, 1)
            pool.memset(ones[:, :], 1.0).then_inc(const_ready, 1)
            pool.wait_ge(const_ready, 4)
            for t in (ident, ident_bf):
                pool.affine_select(out=t[:, :], in_=t[:, :], compare_op=ALU.not_equal, fill=1.0, base=0,
                                   pattern=[[-1, P]], channel_multiplier=1).then_inc(const_ready, 1)
            pool.affine_select(out=mask_bf[:, :], in_=mask_bf[:, :], compare_op=ALU.is_ge,
                               fill=-1e10 * SCALE, base=0, pattern=[[-1, P]],
                               channel_multiplier=1).then_inc(const_ready, 1)

            pool.wait_ge(had_copied, 2)
            src, dst = w2_b, w2_a
            for r in range(3):
                w = D << r
                s = src[:, :].rearrange("p (g two w) -> p g two w", two=2, w=w)
                d = dst[:, :].rearrange("p (g two w) -> p g two w", two=2, w=w)
                if r:
                    pool.wait_ge(w2_summed, 2 * r)
                pool.tensor_tensor(d[:, :, 0, :], s[:, :, 0, :], s[:, :, 1, :], ALU.add).then_inc(w2_summed, 1)
                pool.tensor_tensor(d[:, :, 1, :], s[:, :, 0, :], s[:, :, 1, :], ALU.subtract
                                   ).then_inc(w2_summed, 1)
                src, dst = dst, src

            pool.wait_ge(w2_hi_done, 1)
            pool.tensor_tensor(w2_lo, w2_a[:, :], w2_hi.bitcast(F32), ALU.subtract).then_inc(w2_lo_done, 1)

            def split_qkv():
                pool.tensor_tensor(wqkv_hi[:, :, :], w_raw[:, 0:3, :], ones[:, :].to_broadcast([P, 3, D]), ALU.mult).then_inc(pool_hi, 1)

            def split_qkv_lo():
                pool.tensor_tensor(wqkv_lo[:, :, :], w_raw[:, 0:3, :], wqkv_hi[:, :, :].bitcast(F32),
                                   ALU.subtract).then_inc(wqkv_split, 1)

            def split_wo():
                pool.tensor_tensor(wo_hi[:, :], w_raw[:, 3, :], ones[:, :].to_broadcast([P, D]), ALU.mult).then_inc(pool_hi, 1)

            def split_wo_lo():
                pool.tensor_tensor(wo_lo[:, :], w_raw[:, 3, :], wo_hi[:, :].bitcast(F32),
                                   ALU.subtract).then_inc(wo_split, 1)

            pool.wait_ge(head_loaded, 16)
            split_qkv()
            pool.wait_ge(pool_hi, 1)
            split_qkv_lo()
            split_wo()
            pool.wait_ge(pool_hi, 2)
            split_wo_lo()

            def add_outputs(h):
                for c in range(CHUNKS):
                    pool.wait_ge(shared, CHUNKS * h + c + 1 + O_FREE)
                    pool.tensor_tensor(acc[:, 2 * c:2 * c + 2, :], share[:, c % 2, :, :],
                                       acc[:, 2 * c:2 * c + 2, :], ALU.add).then_inc(out_added, 1)

            pool.wait_ge(ffn_added, PER_Q * QUARTERS + 1)
            pool.memset(share[:, 0, 0, 0:4], 0.0).then_inc(out_added, SHARE_FREE)
            with pool.Fori(0, HEADS - 1) as h:
                pool.wait_ge(head_loaded, 16 * h + 32)
                pool.wait_ge(ring_filled, filled(h, ("V", QUARTERS - 1)))
                split_qkv()
                pool.wait_ge(pool_hi, 2 * h + 3)
                split_qkv_lo()
                add_outputs(h)
                pool.wait_ge(wo_product, CHUNKS * h + CHUNKS)
                split_wo()
                pool.wait_ge(pool_hi, 2 * h + 4)
                split_wo_lo()
            add_outputs(HEADS - 1)

        @block.scalar
        def _(act):
            for i in range(2):
                act.wait_ge(had_product, 2 * i + 2)
                act.activation(w2_b[:, i * 1024:(i + 1) * 1024], ps[:, i * 1024:(i + 1) * 1024], ACT.Copy,
                               scale=HAD_SCALE).then_inc(had_copied, 1)

            for c in range(QUARTERS):
                act.wait_ge(inv_done, c + 1)
                act.activation(rstd[:, c * PER_Q:(c + 1) * PER_Q], inv_var[:, c * PER_Q:(c + 1) * PER_Q],
                               ACT.Sqrt).then_inc(rstd_done, 1)
            def xt_to_hi(p):
                act.wait_ge(xn_transposed, p + 1)
                act.copy(xt_hi[:, :, p * 2 * P:(p + 1) * 2 * P],
                         bank(TRANS + p % 4).rearrange("p (k q) -> p k q", k=KD)).then_inc(xt_hi_done, 1)

            for p in range(5):
                xt_to_hi(p)
            act.wait_ge(w1_loaded, 16)
            act.copy(w1_hi, w1_raw).then_inc(w13_hi_done, 1)
            for p in range(5, TILES // 2):
                xt_to_hi(p)
            act.wait_ge(w3_loaded, 16)
            act.copy(w3_hi, w3_raw).then_inc(w13_hi_done, 1)
            act.wait_ge(w2_summed, 6)
            act.copy(w2_hi, w2_a[:, :]).then_inc(w2_hi_done, 1)
            act.wait_ge(w13_lo_done, 2)

            def hidden_to_hi(c, t):
                act.wait_ge(hidden_done, HT * c + t + 1 + G_FREE)
                act.copy(hid_hi[:, (t % 4) * BANK:(t % 4 + 1) * BANK], hidden[t % 2]).then_inc(hid_hi_done, 1)

            act.activation(table_use[:, 0:1], ones[:, :], ACT.Silu)
            with act.Fori(0, QUARTERS) as c:
                for t in range(HT):
                    act.wait_ge(gate_product, HT * c + t + 1)
                    act.activation(gate[t % 2], bank(2 * (t % 2)), ACT.Silu).then_inc(gate_done, 1)
                    if t >= 1:
                        hidden_to_hi(c, t - 1)
                hidden_to_hi(c, HT - 1)

            def project(hh, first, last):
                for i in range(first, last):
                    b = i % QUARTERS
                    act.wait_ge(projected, PROJ * hh + i + 1)
                    act.activation((k_hi, q_hi)[i // QUARTERS][:, b * BANK:(b + 1) * BANK], bank(b), ACT.Copy,
                                   scale=(1.0, SCALE)[i // QUARTERS]).then_inc(proj_hi, 1)

            def head(h, last):
                def p_to_hi(j, g):
                    n = min(4, j + 1 - 4 * g)
                    act.wait_ge(ring_filled, filled(h, (j, g)))
                    act.copy(pt_hi4[:, (j // 2) % 2, 4 * g:4 * g + n, (j % 2) * P:(j % 2 + 1) * P],
                             bank(ring_bank((j, g)), 0, n * P).rearrange("p (t q) -> p t q", q=P)
                             ).then_inc(ring_hi, 1)

                def v_to_hi(s):
                    for item in v_items(s):
                        if item[0] == "VT":
                            b = item[1]
                            act.wait_ge(ring_filled, filled(h, item))
                            act.copy(v_hi[:, b * BANK:(b + 1) * BANK], bank(ring_bank(item))).then_inc(ring_hi, 1)

                def exponential(j, e):
                    b, end = exps_of(j)[e]
                    n = min(end * BANK, (j + 1) * P) - b * BANK
                    at = score_bank(j, b) * BANK
                    if e == 0:
                        act.wait_ge(negmaxed, TILES * h + j + 1)
                    act.activation(probs[:, j % 2, b * BANK:b * BANK + n], ps[:, at:at + n], ACT.Exp,
                                   bias=neg_max[:, j:j + 1], accum_out=row_part[:, j, e:e + 1]
                                   ).then_inc(exped, 1)

                def z_to_hi(c):
                    act.wait_ge(z_product, CHUNKS * h + c + 1)
                    act.copy(z_hi[:, :], bank(Z, 0, CHUNK_Q)).then_inc(z_hi_done, 1)

                def output(c):
                    act.wait_ge(rcp_done, CHUNKS * h + c + 1)
                    act.wait_ge(out_added, CHUNKS * h + c - 1 + SHARE_FREE)
                    act.wait_ge(wo_product, CHUNKS * h + c + 1)
                    for t in range(2):
                        j = 2 * c + t
                        ins = act.activation(share[:, c % 2, t, :],
                                             bank(ring_bank(("O", c)), t * D, (t + 1) * D), ACT.Copy,
                                             scale=row_rcp[:, j:j + 1])
                    ins.then_inc(shared, 1)

                for s in range(TILES):
                    nt = banks_of(s - 1) if s else 0
                    z = s >= 5 and s % 2
                    if z:
                        z_to_hi((s - 5) // 2)
                    if s == 5:
                        v_to_hi(4)
                    if nt:
                        p_to_hi(s - 1, 0)
                    for g in range(1, min(nt, 3)):
                        p_to_hi(s - 1, g)
                    exponential(s, 0)
                    if nt == 4:
                        p_to_hi(s - 1, 3)
                    if len(exps_of(s)) == 2:
                        exponential(s, 1)
                    if z:
                        output((s - 5) // 2)
                    if s != 4:
                        v_to_hi(s)
                z_to_hi(CHUNKS - 2)
                p_to_hi(TILES - 1, 0)
                p_to_hi(TILES - 1, 1)
                if not last:
                    project(h + 1, 0, 2)
                output(CHUNKS - 2)
                p_to_hi(TILES - 1, 2)
                if not last:
                    project(h + 1, 2, QUARTERS - 1)
                p_to_hi(TILES - 1, 3)
                if not last:
                    project(h + 1, QUARTERS - 1, QUARTERS)
                z_to_hi(CHUNKS - 1)
                if not last:
                    project(h + 1, QUARTERS, PROJ)
                output(CHUNKS - 1)

            act.activation(table_use[:, 1:2], ones[:, :], ACT.Exp)
            project(0, 0, PROJ)
            with act.Fori(0, HEADS - 1) as h:
                head(h, False)
            head(HEADS - 1, True)

        @block.vector
        def _(dve):
            def normalize(p):
                dve.wait_ge(rstd_done, p // 2 + 1)
                if p >= 2:
                    dve.wait_ge(xn_transposed, p - 1)
                for i in (2 * p, 2 * p + 1):
                    dve.tensor_scalar(xn[:, i % 4, :], acc[:, i, :], mean_var[:, i, 0:1], rstd[:, i:i + 1],
                                      ALU.subtract, ALU.mult).then_inc(xn_done, 1)

            def xt_to_lo(p):
                dve.wait_ge(xt_hi_done, p + 1)
                sl = slice(p * 2 * P, (p + 1) * 2 * P)
                dve.tensor_tensor(xt_lo[:, :, sl], bank(TRANS + p % 4).rearrange("p (k q) -> p k q", k=KD),
                                  xt_hi[:, :, sl].bitcast(F32), ALU.subtract).then_inc(xt_lo_done, 1)

            for c in range(QUARTERS):
                q = slice(c * PER_Q, (c + 1) * PER_Q)
                dve.wait_ge(x_loaded[c], 16)
                for t in range(PER_Q):
                    dve.bn_stats(stats[:, t, :], acc[:, c * PER_Q + t, :]).then_inc(stats_done, 1)
                dve.wait_ge(stats_done, PER_Q * (c + 1))
                for t in range(PER_Q):
                    dve.bn_aggr(mean_var[:, c * PER_Q + t, :], stats[:, t, :]).then_inc(aggr_done, 1)
                dve.wait_ge(aggr_done, PER_Q * (c + 1))
                dve.tensor_scalar(inv_var[:, q], mean_var[:, q, 1], EPS, None, ALU.add).then_inc(eps_done, 1)
                dve.wait_ge(eps_done, c + 1)
                dve.reciprocal(inv_var[:, q], inv_var[:, q]).then_inc(inv_done, 1)
            normalize(0)
            for p in range(1, TILES // 2):
                normalize(p)
                xt_to_lo(p - 1)
                if p == 5:
                    dve.wait_ge(w13_hi_done, 1)
                    dve.tensor_tensor(w1_lo, w1_raw, w1_hi.bitcast(F32), ALU.subtract).then_inc(w13_lo_done, 1)
            xt_to_lo(TILES // 2 - 1)
            dve.wait_ge(w13_hi_done, 2)
            dve.tensor_tensor(w3_lo, w3_raw, w3_hi.bitcast(F32), ALU.subtract).then_inc(w13_lo_done, 1)
            dve.wait_ge(had_copied, 2)
            dve.memset(bank_max[:, 1, :], 0.0).then_inc(hidden_done, G_FREE)
            dve.memset(bank_max[:, 2, :], 0.0).then_inc(hid_lo_done, G_FREE)
            dve.memset(bank_max[:, 0, :], 0.0).then_inc(ffn_added, 1)

            def hidden_to_lo(c, t):
                sl = slice((t % 4) * BANK, (t % 4 + 1) * BANK)
                dve.wait_ge(hid_hi_done, HT * c + t + 1)
                dve.tensor_tensor(hid_lo[:, sl], hidden[t % 2], hid_hi[:, sl].bitcast(F32),
                                  ALU.subtract).then_inc(hid_lo_done, 1)

            with dve.Fori(0, QUARTERS) as c:
                for t in range(HT):
                    dve.wait_ge(up_product, HT * c + t + 1)
                    dve.wait_ge(gate_done, HT * c + t + 1)
                    dve.wait_ge(hid_lo_done, HT * c + t - 1 + G_FREE)
                    dve.tensor_tensor(hidden[t % 2], gate[t % 2], bank(2 * (t % 2) + 1), ALU.mult
                                      ).then_inc(hidden_done, 1)
                    if t >= 1:
                        hidden_to_lo(c, t - 1)
                hidden_to_lo(c, HT - 1)
                for t in range(PER_Q):
                    a = acc[:, bass.ds(c * PER_Q + t, 1), :].rearrange("p a d -> p (a d)")
                    dve.wait_ge(ffn_product, PER_Q * c + t + 1)
                    dve.tensor_tensor(a, bank(TRANS + t, 0, D), a, ALU.add).then_inc(ffn_added, 1)

            dve.wait_ge(ffn_added, PER_Q * QUARTERS + 1)
            dve.memset(bank_max[:, 0, :], 0.0).then_inc(ring_freed, R_FREE)
            dve.memset(bank_max[:, 1, :], 0.0).then_inc(z_lo_done, Z_FREE)
            dve.memset(bank_max[:, 2, :], 0.0).then_inc(shared, O_FREE)

            def project(hh, first, last):
                for i in range(first, last):
                    b = i % QUARTERS
                    hi, lo = ((k_hi, k_lo), (q_hi, q_lo))[i // QUARTERS]
                    sl = slice(b * BANK, (b + 1) * BANK)
                    dve.wait_ge(proj_hi, PROJ * hh + i + 1)
                    if i < QUARTERS:
                        dve.tensor_tensor(lo[:, sl], bank(b), hi[:, sl].bitcast(F32),
                                          ALU.subtract).then_inc(proj_lo, 1)
                    else:
                        dve.scalar_tensor_tensor(out=lo[:, sl], in0=bank(b), scalar=SCALE,
                                                 in1=hi[:, sl].bitcast(F32), op0=ALU.mult,
                                                 op1=ALU.subtract).then_inc(proj_lo, 1)

            def head(h, last):
                def maximum(j, b):
                    one = banks_of(j) == 1
                    at = score_bank(j, b) * BANK
                    dve.wait_ge(scored, HEAD_BANKS * h + TB[j] + b + 1)
                    dst = neg_max[:, j:j + 1] if one else bank_max[:, j, b:b + 1]
                    dve.tensor_reduce(dst, ps[:, at:at + min(BANK, (j + 1) * P - b * BANK)], AX_X, ALU.max,
                                      negate=one).then_inc(negmaxed if one else maxed, 1)

                def negated_maximum(j):
                    if banks_of(j) > 1:
                        dve.wait_ge(maxed, (TB[TILES] - 4) * h + TB[j + 1] - 4)
                        dve.tensor_reduce(neg_max[:, j:j + 1], bank_max[:, j, 0:banks_of(j)], AX_X, ALU.max,
                                          negate=True).then_inc(negmaxed, 1)

                def p_to_lo(j, g):
                    n = min(4, j + 1 - 4 * g)
                    dve.wait_ge(ring_hi, split_hi(h, (j, g)))
                    where = (slice(None), (j // 2) % 2, slice(4 * g, 4 * g + n), slice((j % 2) * P, (j % 2 + 1) * P))
                    dve.tensor_tensor(pt_lo4[where],
                                      bank(ring_bank((j, g)), 0, n * P).rearrange("p (t q) -> p t q", q=P),
                                      pt_hi4[where].bitcast(F32), ALU.subtract).then_inc(ring_freed, 1)

                def v_out(s):
                    for item in v_items(s):
                        b = item[1]
                        sl = slice(b * BANK, (b + 1) * BANK)
                        if item[0] == "V":
                            dve.wait_ge(ring_filled, filled(h, item))
                            dve.tensor_copy(v_raw[b % 2], bank(ring_bank(item))).then_inc(ring_freed, 1)
                        else:
                            dve.wait_ge(ring_hi, split_hi(h, item))
                            dve.tensor_tensor(v_lo[:, sl], bank(ring_bank(item)), v_hi[:, sl].bitcast(F32),
                                              ALU.subtract).then_inc(ring_freed, 1)

                def z_to_lo(c):
                    dve.wait_ge(z_hi_done, CHUNKS * h + c + 1)
                    dve.tensor_tensor(z_lo[:, :], bank(Z, 0, CHUNK_Q), z_hi[:, :].bitcast(F32),
                                      ALU.subtract).then_inc(z_lo_done, 1)

                def reciprocals(c):
                    j = 2 * c
                    dve.wait_ge(exped, EX[TILES] * h + EX[j + 2])
                    if len(exps_of(j)) == 1:
                        dve.reciprocal(row_rcp[:, j:j + 2], row_part[:, j:j + 2, 0]).then_inc(rcp_done, 1)
                    else:
                        dve.tensor_tensor(row_sum[:, j:j + 2], row_part[:, j:j + 2, 0], row_part[:, j:j + 2, 1],
                                          ALU.add).then_inc(summed, 1)
                        dve.wait_ge(summed, (CHUNKS // 2) * h + c - CHUNKS // 2 + 1)
                        dve.reciprocal(row_rcp[:, j:j + 2], row_sum[:, j:j + 2]).then_inc(rcp_done, 1)

                for s in range(TILES):
                    nt, nb = banks_of(s - 1) if s else 0, banks_of(s)
                    early = 1 if nb > 2 else 0
                    maximum(s, 0)
                    if s >= 5 and s % 2:
                        z_to_lo((s - 5) // 2)
                        reciprocals((s - 5) // 2)
                    if s == 5:
                        v_out(4)
                    if nb > 1:
                        maximum(s, 1)
                    for g in range(early):
                        p_to_lo(s - 1, g)
                    for b in range(2, nb):
                        maximum(s, b)
                    negated_maximum(s)
                    for g in range(early, nt):
                        p_to_lo(s - 1, g)
                    if s != 4:
                        v_out(s)
                z_to_lo(CHUNKS - 2)
                p_to_lo(TILES - 1, 0)
                p_to_lo(TILES - 1, 1)
                reciprocals(CHUNKS - 2)
                reciprocals(CHUNKS - 1)
                if not last:
                    project(h + 1, 0, 2)
                p_to_lo(TILES - 1, 2)
                if not last:
                    project(h + 1, 2, QUARTERS - 1)
                p_to_lo(TILES - 1, 3)
                if not last:
                    project(h + 1, QUARTERS - 1, QUARTERS)
                z_to_lo(CHUNKS - 1)
                if not last:
                    project(h + 1, QUARTERS, PROJ)

            project(0, 0, PROJ)
            with dve.Fori(0, HEADS - 1) as h:
                head(h, False)
            head(HEADS - 1, True)

        @block.tensor
        def _(pe):
            def mm3(dst, a, b, start, stop):
                pe.matmul(dst, a[0], b[0], start=start, stop=False, skip_group_check=True)
                pe.matmul(dst, a[0], b[1], start=False, stop=False, skip_group_check=True)
                return pe.matmul(dst, a[1], b[0], start=False, stop=stop, skip_group_check=True)

            pe.wait_ge(had_loaded, 16)
            pe.wait_ge(w2_loaded, 16)
            for i in range(4):
                pe.matmul(bank(i), had, w2_a[:, i * BANK:(i + 1) * BANK], start=True, stop=True
                          ).then_inc(had_product, 1)

            pe.wait_ge(const_ready, 7)
            for p in range(TILES // 2):
                pe.wait_ge(xn_done, 2 * p + 2)
                if p >= 4:
                    pe.wait_ge(xt_lo_done, p - 3)
                for k in range(KD):
                    for t in range(2):
                        i = 2 * p + t
                        ins = pe.transpose(bank(TRANS + p % 4, (2 * k + t) * P, (2 * k + t + 1) * P),
                                           xn[:, i % 4, k * P:(k + 1) * P], ident[:, :])
                ins.then_inc(xn_transposed, 1)

            pe.wait_ge(xt_lo_done, TILES // 2)
            pe.wait_ge(w13_lo_done, 2)

            def down(c, t):
                pe.wait_ge(hid_lo_done, HT * c + t + 1 + G_FREE)
                if t == 0:
                    pe.wait_ge(w2_lo_done, 1)
                    pe.wait_ge(ffn_added, PER_Q * c + 1)
                for q in range(PER_Q):
                    sl = slice((t % 4) * BANK + q * P, (t % 4) * BANK + (q + 1) * P)
                    ins = mm3(bank(TRANS + q, 0, D), (hid_hi[:, sl], hid_lo[:, sl]),
                              (w2_hi[:, t * D:(t + 1) * D], w2_lo[:, t * D:(t + 1) * D]), t == 0, t == HT - 1)
                    if t == HT - 1:
                        ins.then_inc(ffn_product, 1)

            with pe.Fori(0, QUARTERS) as c:
                for t in range(HT):
                    pe.wait_ge(hidden_done, HT * c + t - 1 + G_FREE)
                    for b, hi, lo, done in ((0, w1_hi, w1_lo, gate_product), (1, w3_hi, w3_lo, up_product)):
                        for k in range(KD):
                            sl = slice(k * HID + t * P, k * HID + (t + 1) * P)
                            xs = (xt_hi[:, k, bass.ds(c * BANK, BANK)], xt_lo[:, k, bass.ds(c * BANK, BANK)])
                            ins = mm3(bank(2 * (t % 2) + b), (hi[:, sl], lo[:, sl]), xs, k == 0, k == KD - 1)
                        ins.then_inc(done, 1)
                    if t >= 2:
                        down(c, t - 2)
                down(c, HT - 2)
                down(c, HT - 1)

            def project_slice(dst, w, sl):
                for k in range(KD):
                    ws = slice(k * P, (k + 1) * P)
                    ins = mm3(dst, (wqkv_hi[:, w, ws], wqkv_lo[:, w, ws]),
                              (xt_hi[:, k, sl], xt_lo[:, k, sl]), k == 0, k == KD - 1)
                return ins

            def project(hh, first, last):
                for i in range(first, last):
                    b = i % QUARTERS
                    if i >= QUARTERS:
                        pe.wait_ge(proj_lo, PROJ * hh + i - QUARTERS + 1)
                    project_slice(bank(b), 1 - i // QUARTERS, slice(b * BANK, (b + 1) * BANK)
                                  ).then_inc(projected, 1)

            def head(h, last):
                def scores(j, b):
                    if j < 4:
                        pe.wait_ge(proj_lo, PROJ * h + QUARTERS + j + 1)
                    elif b == 0 or exp_of(*BANK_OF[TB[j] + b - 4]) != exp_of(*BANK_OF[TB[j] + b - 5]):
                        pe.wait_ge(exped, EX[TILES] * h + exp_of(*BANK_OF[TB[j] + b - 4]) + 1)
                    n = min(BANK, (j + 1) * P - b * BANK)
                    qs, ks = slice(j * P, (j + 1) * P), slice(b * BANK, b * BANK + n)
                    dst = bank(score_bank(j, b), 0, n)
                    diagonal = b == banks_of(j) - 1
                    ins = mm3(dst, (q_hi[:, qs], q_lo[:, qs]), (k_hi[:, ks], k_lo[:, ks]), True, not diagonal)
                    if diagonal:
                        ins = pe.matmul(bank(score_bank(j, b), n - P, n), ident_bf[:, :], mask_bf[:, :],
                                        start=False, stop=True, skip_group_check=True)
                    ins.then_inc(scored, 1)

                def ring_wait(item):
                    n = ITEM[item] - RING
                    hh, before = (h, ITEMS[n]) if n >= 0 else (h - 1, ITEMS[n] or ITEMS[n - RING])
                    if before[0] == "O":
                        pe.wait_ge(shared, CHUNKS * hh + before[1] + 1 + O_FREE)
                    else:
                        pe.wait_ge(ring_freed, freed(hh, before))

                def transposes(j, g):
                    if g == 0 or exp_of(j, g) != exp_of(j, g - 1):
                        pe.wait_ge(exped, EX[TILES] * h + exp_of(j, g) + 1)
                    ring_wait((j, g))
                    for i in range(4 * g, min(4 * g + 4, j + 1)):
                        ins = pe.transpose(bank(ring_bank((j, g)), (i % 4) * P, (i % 4 + 1) * P),
                                           probs[:, j % 2, i * P:(i + 1) * P], ident[:, :])
                    ins.then_inc(ring_filled, 1)

                def v(s):
                    for item in v_items(s):
                        what, b = item
                        ring_wait(item)
                        if what == "V":
                            project_slice(bank(ring_bank(item)), 2, slice(b * BANK, (b + 1) * BANK)
                                          ).then_inc(ring_filled, 1)
                        else:
                            pe.wait_ge(ring_freed, freed(h, ("V", b)))
                            for t in range(PER_Q):
                                ins = pe.transpose(bank(ring_bank(item), t * P, (t + 1) * P),
                                                   v_raw[b % 2][:, t * P:(t + 1) * P], ident[:, :])
                            ins.then_inc(ring_filled, 1)

                def weighted_sum(c, first, last):
                    if first == 0:
                        pe.wait_ge(z_lo_done, CHUNKS * h + c + Z_FREE)
                    for i in range(first, last):
                        if i % 4 == 0 or i == first:
                            pe.wait_ge(ring_freed, freed(h, (2 * c + 1, i // 4)))
                        lo = P if i == 2 * c + 1 else 0
                        ks = slice(i * P, (i + 1) * P)
                        ins = mm3(bank(Z, lo, CHUNK_Q), (v_hi[:, ks], v_lo[:, ks]),
                                  (pt_hi4[:, c % 2, i, lo:CHUNK_Q], pt_lo4[:, c % 2, i, lo:CHUNK_Q]),
                                  i == 0, i == 2 * c + 1)
                    if last == 2 * c + 2:
                        ins.then_inc(z_product, 1)

                def output(c):
                    pe.wait_ge(z_lo_done, CHUNKS * h + c + 1 + Z_FREE)
                    ring_wait(("O", c))
                    if c == 0:
                        pe.wait_ge(wo_split, h + 1)
                    for t in range(2):
                        qs = slice(t * P, (t + 1) * P)
                        ins = mm3(bank(ring_bank(("O", c)), t * D, (t + 1) * D), (z_hi[:, qs], z_lo[:, qs]),
                                  (wo_hi[:, :], wo_lo[:, :]), True, True)
                    ins.then_inc(wo_product, 1)

                for s in range(TILES):
                    nt = banks_of(s - 1) if s else 0
                    done = [0, 0]
                    for what in ORDERS[s]:
                        n = what == "t"
                        (scores, transposes)[n](s - n, done[n])
                        done[n] += 1
                    v(s)
                    part = []
                    if s >= 3 and s % 2:
                        c = (s - 3) // 2
                        part = [(c, 0, (c + 1) // 2), (c, (c + 1) // 2, c + 1)]
                    elif s >= 4:
                        c = (s - 4) // 2
                        part = [(c, c + 1, c + 1 + (c + 1) // 2), (c, c + 1 + (c + 1) // 2, 2 * c + 2)]
                    for n, (c, a, b) in enumerate(part):
                        if a < b:
                            weighted_sum(c, a, b)
                        if n == 0 and nt == 4:
                            transposes(s - 1, 3)
                        if n == 1 and s >= 5 and s % 2:
                            output((s - 5) // 2)
                c = CHUNKS - 1
                weighted_sum(c - 1, c, 2 * c)
                transposes(TILES - 1, 0)
                transposes(TILES - 1, 1)
                if not last:
                    pe.wait_ge(wqkv_split, h + 2)
                    pe.wait_ge(exped, EX[TILES] * h + EX[TILES])
                    project(h + 1, 0, 1)
                if not last:
                    project(h + 1, 1, 2)
                output(c - 1)
                transposes(TILES - 1, 2)
                if not last:
                    project(h + 1, 2, QUARTERS - 1)
                transposes(TILES - 1, 3)
                if not last:
                    project(h + 1, QUARTERS - 1, QUARTERS)
                weighted_sum(c, 0, c + 1)
                weighted_sum(c, c + 1, 2 * c + 2)
                if not last:
                    project(h + 1, QUARTERS, PROJ)
                output(c)

            pe.wait_ge(wqkv_split, 1)
            pe.wait_ge(hidden_done, HT * QUARTERS + G_FREE)
            project(0, 0, PROJ)
            with pe.Fori(0, HEADS - 1) as h:
                head(h, False)
            head(HEADS - 1, True)


def kernel(L0_attn_x, L0_attn_W_K, L0_attn_W_Q, L0_attn_W_V, L0_attn_W_O, L0_ffn_W1, L0_ffn_W2, L0_ffn_W3):
    import numpy as np
    import concourse.bacc as bacc
    from concourse.bass_utils import run_bass_kernel_spmd

    x = np.ascontiguousarray(L0_attn_x)[0]
    heads, dh, d = L0_attn_W_Q.shape
    hid = L0_ffn_W1.shape[0]

    def by_model(w):
        return np.asarray(w).T.reshape(d // P, P, -1).transpose(1, 0, 2)

    def head_weights(w):
        return np.asarray(w).transpose(0, 2, 1).reshape(heads, d // P, P, dh).transpose(0, 2, 1, 3).reshape(
            heads, P, -1)

    w_o = np.asarray(L0_attn_W_O).T.reshape(heads, dh, d)
    h128 = np.array([[1 - 2 * (bin(i & j).count("1") & 1) for j in range(P)] for i in range(P)], np.float32)
    arrays = {
        "x": x,
        "w_heads": np.ascontiguousarray(np.stack(
            [head_weights(L0_attn_W_Q), head_weights(L0_attn_W_K), head_weights(L0_attn_W_V), w_o], axis=2)),
        "w1t": np.ascontiguousarray(by_model(L0_ffn_W1)),
        "w3t": np.ascontiguousarray(by_model(L0_ffn_W3)),
        "w2t": np.ascontiguousarray(np.asarray(L0_ffn_W2).T.reshape(hid // P, P, d).transpose(1, 0, 2)),
        "hadamard": h128,
    }
    nc = bacc.Bacc("TRN2", target_bir_lowering=False, num_devices=1)
    args = [nc.dram_tensor(n, a.shape, mybir.dt.from_np(a.dtype), kind="ExternalInput").ap()
            for n, a in arrays.items()]
    out = nc.dram_tensor("out", x.shape, F32, kind="ExternalOutput").ap()
    attention_ffn_kernel(nc, *args, out)
    r = run_bass_kernel_spmd(nc, [arrays], core_ids=[0])
    return r.results[0]["out"].reshape(L0_attn_x.shape)
```

```python
from contextlib import ExitStack

import concourse.bass as bass
from concourse import mybir

F32 = mybir.dt.float32
F32R = mybir.dt.float32r
ALU = mybir.AluOpType
ACT = mybir.ActivationFunctionType
AX_X = mybir.AxisListType.X

P = 128
BANK = 512
CHUNK_Q = 256
EPS = 1e-5


def attention_ffn_kernel(nc, x, w_heads, w1t, w3t, w2t, hadamard, out):
    S, D = x.shape
    HEADS = w_heads.shape[0]
    HID = w1t.shape[2]
    KD = D // P
    TILES = S // P
    QUARTERS = S // BANK
    PER_Q = BANK // P
    HT = HID // P
    CHUNKS = S // CHUNK_Q
    SCALE = float(P) ** -0.5
    HAD_SCALE = float(HID) ** -0.5
    assert D == 256 and S == 2048 and HT == 8 and KD == 2

    def banks_of(j):
        return j // PER_Q + 1

    SCORE_BANKS = 4
    ORDERS = (["s"] + ["st"] * 3 + ["sst"] + ["sstt"] * 3
              + ["ssstt", "stsstt", "sssttt", "stsstt"] + ["stsstst"] * 4)
    assert TILES == len(ORDERS)

    def score_bank(j, b):
        return (TB[j] + b) % SCORE_BANKS

    def exps_of(j):
        n = banks_of(j)
        if n <= 2:
            return [(0, n)]
        if score_bank(j, 1) == 0 or score_bank(j, 2) == 0:
            cut = 1 if score_bank(j, 1) == 0 else 2
        else:
            cut = 1 if n == 3 or j % 2 == 0 else 2
        return [(0, cut), (cut, n)]

    TB = [sum(banks_of(i) for i in range(j)) for j in range(TILES + 1)]
    HEAD_BANKS = TB[TILES]
    assert HEAD_BANKS % SCORE_BANKS == 0

    def exp_of(j, b):
        return EX[j] + [lo <= b < hi for lo, hi in exps_of(j)].index(True)

    def v_items(s):
        return ([("V", s)] if s < QUARTERS else []) + ([("VT", s - 1)] if 1 <= s <= QUARTERS else [])

    EX = [sum(len(exps_of(i)) for i in range(j)) for j in range(TILES + 1)]

    BANK_OF = [(j, b) for j in range(TILES) for b in range(banks_of(j))]

    RING = 3
    ITEMS = []
    for slot in range(TILES):
        nt = banks_of(slot - 1) if slot else 0
        ITEMS += [(slot - 1, g) for g in range(min(nt, 3))] + v_items(slot)
        ITEMS += [(slot - 1, 3)] if nt == 4 else []
        ITEMS += [("O", (slot - 5) // 2)] if slot >= 5 and slot % 2 else []
    ITEMS += [(TILES - 1, 0), (TILES - 1, 1), ("O", CHUNKS - 2), (TILES - 1, 2), (TILES - 1, 3),
              ("O", CHUNKS - 1), None]
    ITEM = {item: n for n, item in enumerate(ITEMS)}
    SPLIT_ITEMS = [item for item in ITEMS if item and item[0] not in ("V", "O")]
    FREED_ITEMS = [item for item in ITEMS if item and item[0] != "O"]
    assert len(ITEMS) % RING == 0

    with ExitStack() as ctx:
        def sb(name, shape, dt):
            return ctx.enter_context(nc.sbuf_tensor(name, shape, dt))

        def sem(name):
            return ctx.enter_context(nc.semaphore(name))

        ps = ctx.enter_context(nc.psum_tensor("ps", [P, 8 * BANK], F32))

        def bank(b, lo=0, hi=BANK):
            return ps[:, b * BANK + lo:b * BANK + hi]

        TRANS, Z = 4, 7

        acc = sb("acc", [P, TILES, D], F32)
        xt_hi = sb("xt_hi", [P, KD, S], F32R)
        xt_lo = sb("xt_lo", [P, KD, S], F32R)
        ident = sb("ident", [P, P], F32)
        wait_mark = sb("wait_mark", [P, 1], F32)
        ones = sb("ones", [P, 1], F32)
        table_use = sb("table_use", [P, 3], F32)

        k_hi, k_lo = sb("k_hi", [P, S], F32R), sb("k_lo", [P, S], F32R)
        q_hi, q_lo = sb("q_hi", [P, S], F32R), sb("q_lo", [P, S], F32R)
        v_hi, v_lo = sb("v_hi", [P, S], F32R), sb("v_lo", [P, S], F32R)
        pt_hi = sb("pt_hi", [P, 2 * TILES * CHUNK_Q], F32R)
        pt_lo = sb("pt_lo", [P, 2 * TILES * CHUNK_Q], F32R)
        probs = sb("probs", [P, 2, S], F32)
        z_hi, z_lo = sb("z_hi", [P, CHUNK_Q], F32R), sb("z_lo", [P, CHUNK_Q], F32R)
        w_raw = sb("w_raw", [P, 4, D], F32)
        wqkv_hi, wqkv_lo = sb("wqkv_hi", [P, 3, D], F32R), sb("wqkv_lo", [P, 3, D], F32R)
        wo_hi, wo_lo = sb("wo_hi", [P, D], F32R), sb("wo_lo", [P, D], F32R)
        bank_max = sb("bank_max", [P, TILES, 4], F32)
        neg_max = sb("neg_max", [P, TILES], F32)

        stats = sb("stats", [P, PER_Q, 6], F32)
        mean_var = sb("mean_var", [P, TILES, 2], F32)
        inv_var = sb("inv_var", [P, TILES], F32)
        rstd = sb("rstd", [P, TILES], F32)
        w2_a, w2_b = sb("w2_a", [P, HT * D], F32), sb("w2_b", [P, HT * D], F32)
        had = w2_b[:, HT * D - P:HT * D]
        share = w2_a[:, 0:4 * D].rearrange("p (b t d) -> p b t d", b=2, t=2)
        row_part = w2_b[:, 0:2 * TILES].rearrange("p (t e) -> p t e", e=2)
        v_raw = [w2_b[:, (1 + i) * BANK:(2 + i) * BANK] for i in range(2)]
        mask = w2_b[:, 3 * BANK:4 * BANK]
        row_sum, row_rcp = w2_b[:, 2 * TILES:3 * TILES], w2_b[:, 3 * TILES:4 * TILES]
        xn = w_raw

        def region(t, at, n):
            return t[:, at * 2048:at * 2048 + n]

        w1_hi, w3_hi, w2_hi, hid_hi = (region(pt_hi, i, 2048) for i in range(4))
        w1_lo, w3_lo, w2_lo, hid_lo = (region(pt_lo, i, 2048) for i in range(4))
        w1_raw, w3_raw = probs[:, 0, :], probs[:, 1, :]
        gate = [probs[:, 0, i * BANK:(i + 1) * BANK] for i in range(2)]
        hidden = [probs[:, 1, i * BANK:(i + 1) * BANK] for i in range(2)]

        pt_hi4 = pt_hi[:, :].rearrange("p (b t q) -> p b t q", b=2, t=TILES)
        pt_lo4 = pt_lo[:, :].rearrange("p (b t q) -> p b t q", b=2, t=TILES)

        x_loaded = [sem(f"x_loaded{i}") for i in range(QUARTERS)]
        w1_loaded, w3_loaded = sem("w1_loaded"), sem("w3_loaded")
        w2_loaded, had_loaded = sem("w2_loaded"), sem("had_loaded")
        head_loaded = sem("head_loaded")
        out_stored = sem("out_stored")
        const_ready, mask_ready = sem("const_ready"), sem("mask_ready")
        stats_done, aggr_done, eps_done, inv_done = (
            sem("stats_done"), sem("aggr_done"), sem("eps_done"), sem("inv_done"))
        rstd_done, xn_done, xn_transposed = sem("rstd_done"), sem("xn_done"), sem("xn_transposed")
        xt_hi_done, xt_lo_done = sem("xt_hi_done"), sem("xt_lo_done")
        had_product, had_copied, w2_summed = sem("had_product"), sem("had_copied"), sem("w2_summed")
        w2_hi_done, w2_lo_done = sem("w2_hi_done"), sem("w2_lo_done")
        w13_hi_done, w13_lo_done = sem("w13_hi_done"), sem("w13_lo_done")
        gate_product, up_product = sem("gate_product"), sem("up_product")
        gate_done, hidden_done = sem("gate_done"), sem("hidden_done")
        hid_hi_done, hid_lo_done = sem("hid_hi_done"), sem("hid_lo_done")
        ffn_product, ffn_added = sem("ffn_product"), sem("ffn_added")
        wqkv_split, wo_split, pool_hi = sem("wqkv_split"), sem("wo_split"), sem("pool_hi")
        projected, proj_hi, proj_lo = sem("projected"), sem("proj_hi"), sem("proj_lo")
        scored, maxed, negmaxed, exped = sem("scored"), sem("maxed"), sem("negmaxed"), sem("exped")
        ring_filled, ring_hi, ring_freed = sem("ring_filled"), sem("ring_hi"), sem("ring_freed")
        z_product, z_hi_done, z_lo_done = sem("z_product"), sem("z_hi_done"), sem("z_lo_done")
        wo_product, rcp_done, summed = sem("wo_product"), sem("rcp_done"), sem("summed")
        shared, out_added = sem("shared"), sem("out_added")

        PROJ = 2 * QUARTERS
        G_FREE = 2
        R_FREE = RING
        Z_FREE = 1
        O_FREE = 1
        SHARE_FREE = 2

        def ring_bank(item):
            return TRANS + ITEM[item] % RING

        def filled(h, item):
            return len(FREED_ITEMS) * h + FREED_ITEMS.index(item) + 1

        def split_hi(h, item):
            return len(SPLIT_ITEMS) * h + SPLIT_ITEMS.index(item) + 1

        def freed(h, item):
            return len(FREED_ITEMS) * h + FREED_ITEMS.index(item) + 1 + R_FREE

        PAIRS_AFTER = [(2, 3), (4, 5), (6, 7)] + [()] * (HT - 3)

        block = ctx.enter_context(nc.Block())

        @block.sync
        def _(sp):
            x_v = x.rearrange("(c t p) d -> c p t d", p=P, t=PER_Q)
            out_v = out.rearrange("(c t p) d -> c p t d", p=P, t=2)
            for c in range(QUARTERS):
                sp.dma_start(acc[:, c * PER_Q:(c + 1) * PER_Q, :], x_v[c]).then_inc(x_loaded[c], 16)
                if c == 0:
                    sp.dma_start(had, hadamard).then_inc(had_loaded, 16)
                    sp.dma_start(w2_a[:, :], w2t.rearrange("p t d -> p (t d)")).then_inc(w2_loaded, 16)
                if c == 1:
                    sp.dma_start(w1_raw, w1t.rearrange("p k h -> p (k h)")).then_inc(w1_loaded, 16)
                    sp.dma_start(w3_raw, w3t.rearrange("p k h -> p (k h)")).then_inc(w3_loaded, 16)
            sp.wait_ge(xn_transposed, TILES // 2)
            sp.dma_start(w_raw[:, :, :], w_heads[0]).then_inc(head_loaded, 16)
            with sp.Fori(1, HEADS) as h:
                sp.wait_ge(wo_split, h)
                sp.dma_start(w_raw[:, :, :], w_heads[bass.ds(h, 1)].rearrange("a p c d -> (a p) c d")
                             ).then_inc(head_loaded, 16)
            for c in range(CHUNKS):
                sp.wait_ge(out_added, SHARE_FREE + CHUNKS * (HEADS - 1) + c + 1)
                sp.dma_start(out_v[c], acc[:, 2 * c:2 * c + 2, :]).then_inc(out_stored, 16)
            sp.wait_ge(out_stored, 16 * CHUNKS)

        @block.gpsimd
        def _(pool):
            pool.memset(ident[:, :], 0.0).then_inc(const_ready, 1)
            pool.memset(ones[:, :], 1.0).then_inc(const_ready, 1)
            pool.wait_ge(const_ready, 2)
            pool.affine_select(out=ident[:, :], in_=ident[:, :], compare_op=ALU.not_equal, fill=1.0, base=0,
                               pattern=[[-1, P]], channel_multiplier=1).then_inc(const_ready, 1)

            pool.wait_ge(had_copied, 2)
            src, dst = w2_b, w2_a
            for r in range(3):
                w = D << r
                s = src[:, :].rearrange("p (g two w) -> p g two w", two=2, w=w)
                d = dst[:, :].rearrange("p (g two w) -> p g two w", two=2, w=w)
                if r:
                    pool.wait_ge(w2_summed, 2 * r)
                pool.tensor_tensor(d[:, :, 0, :], s[:, :, 0, :], s[:, :, 1, :], ALU.add).then_inc(w2_summed, 1)
                pool.tensor_tensor(d[:, :, 1, :], s[:, :, 0, :], s[:, :, 1, :], ALU.subtract
                                   ).then_inc(w2_summed, 1)
                src, dst = dst, src

            pool.wait_ge(w2_summed, 6)
            pool.memset(mask, 0.0).then_inc(mask_ready, 1)
            pool.wait_ge(mask_ready, 1)
            pool.affine_select(out=mask[:, BANK - P:], in_=mask[:, BANK - P:], compare_op=ALU.is_ge,
                               fill=-1e10 * SCALE, base=0, pattern=[[-1, P]],
                               channel_multiplier=1).then_inc(mask_ready, 1)

            pool.wait_ge(w2_hi_done, 1)
            pool.tensor_tensor(w2_lo, w2_a[:, :], w2_hi.bitcast(F32), ALU.subtract).then_inc(w2_lo_done, 1)

            def split_qkv():
                pool.tensor_tensor(wqkv_hi[:, :, :], w_raw[:, 0:3, :], ones[:, :].to_broadcast([P, 3, D]),
                                   ALU.mult).then_inc(pool_hi, 1)

            def split_qkv_lo():
                pool.tensor_tensor(wqkv_lo[:, :, :], w_raw[:, 0:3, :], wqkv_hi[:, :, :].bitcast(F32),
                                   ALU.subtract).then_inc(wqkv_split, 1)

            def split_wo():
                pool.tensor_tensor(wo_hi[:, :], w_raw[:, 3, :], ones[:, :].to_broadcast([P, D]),
                                   ALU.mult).then_inc(pool_hi, 1)

            def split_wo_lo():
                pool.tensor_tensor(wo_lo[:, :], w_raw[:, 3, :], wo_hi[:, :].bitcast(F32),
                                   ALU.subtract).then_inc(wo_split, 1)

            pool.wait_ge(head_loaded, 16)
            split_qkv()
            pool.wait_ge(pool_hi, 1)
            split_qkv_lo()
            split_wo()
            pool.wait_ge(pool_hi, 2)
            split_wo_lo()

            def add_outputs(h):
                for c in range(CHUNKS):
                    pool.wait_ge(shared, CHUNKS * h + c + 1 + O_FREE)
                    pool.tensor_tensor(acc[:, 2 * c:2 * c + 2, :], share[:, c % 2, :, :],
                                       acc[:, 2 * c:2 * c + 2, :], ALU.add).then_inc(out_added, 1)

            pool.wait_ge(ffn_added, PER_Q * QUARTERS + 1)
            pool.memset(share[:, 0, 0, 0:4], 0.0).then_inc(out_added, SHARE_FREE)
            with pool.Fori(0, HEADS - 1) as h:
                pool.wait_ge(head_loaded, 16 * h + 32)
                pool.wait_ge(ring_filled, filled(h, ("V", QUARTERS - 1)))
                split_qkv()
                pool.wait_ge(pool_hi, 2 * h + 3)
                split_qkv_lo()
                add_outputs(h)
                pool.wait_ge(wo_product, CHUNKS * h + CHUNKS)
                split_wo()
                pool.wait_ge(pool_hi, 2 * h + 4)
                split_wo_lo()
            add_outputs(HEADS - 1)

        @block.scalar
        def _(act):
            def root(c):
                act.wait_ge(inv_done, c + 1)
                act.activation(rstd[:, c * PER_Q:(c + 1) * PER_Q], inv_var[:, c * PER_Q:(c + 1) * PER_Q],
                               ACT.Sqrt).then_inc(rstd_done, 1)

            def xt_to_hi(p):
                act.wait_ge(xn_transposed, p + 1)
                act.copy(xt_hi[:, :, p * 2 * P:(p + 1) * 2 * P],
                         bank(TRANS + p % 4).rearrange("p (k q) -> p k q", k=KD)).then_inc(xt_hi_done, 1)

            def silu(c, t):
                act.wait_ge(gate_product, HT * c + t + 1)
                act.activation(gate[t % 2], bank(2 * (t % 2)), ACT.Silu).then_inc(gate_done, 1)

            def hidden_to_hi(c, t):
                act.wait_ge(hidden_done, HT * c + t + 1 + G_FREE)
                act.copy(hid_hi[:, (t % 4) * BANK:(t % 4 + 1) * BANK], hidden[t % 2]).then_inc(hid_hi_done, 1)

            act.wait_ge(const_ready, 2)
            act.activation(table_use[:, 0:1], ones[:, :], ACT.Sqrt)
            root(0)
            xt_to_hi(0)
            xt_to_hi(1)
            act.wait_ge(w1_loaded, 16)
            act.copy(w1_hi, w1_raw).then_inc(w13_hi_done, 1)
            for i in range(2):
                act.wait_ge(had_product, 2 * i + 2)
                act.activation(w2_b[:, i * 1024:(i + 1) * 1024], ps[:, i * 1024:(i + 1) * 1024], ACT.Copy,
                               scale=HAD_SCALE).then_inc(had_copied, 1)
            root(1)
            act.wait_ge(w3_loaded, 16)
            act.copy(w3_hi, w3_raw).then_inc(w13_hi_done, 1)
            root(2)
            root(3)
            act.activation(table_use[:, 1:2], ones[:, :], ACT.Silu)

            act.wait_ge(w13_lo_done, 2)
            for t in range(HT):
                silu(0, t)
                for p in PAIRS_AFTER[t]:
                    xt_to_hi(p)
                if t >= 1:
                    hidden_to_hi(0, t - 1)
                if t == 1:
                    act.wait_ge(w2_summed, 6)
                    act.copy(w2_hi, w2_a[:, :]).then_inc(w2_hi_done, 1)
            hidden_to_hi(0, HT - 1)

            with act.Fori(1, QUARTERS) as c:
                for t in range(HT):
                    silu(c, t)
                    if t >= 1:
                        hidden_to_hi(c, t - 1)
                hidden_to_hi(c, HT - 1)

            def project(hh, first, last):
                for i in range(first, last):
                    b = i % QUARTERS
                    act.wait_ge(projected, PROJ * hh + i + 1)
                    act.activation((k_hi, q_hi)[i // QUARTERS][:, b * BANK:(b + 1) * BANK], bank(b), ACT.Copy,
                                   scale=(1.0, SCALE)[i // QUARTERS]).then_inc(proj_hi, 1)

            def head(h, last):
                def p_to_hi(j, g):
                    n = min(4, j + 1 - 4 * g)
                    act.wait_ge(ring_filled, filled(h, (j, g)))
                    act.copy(pt_hi4[:, (j // 2) % 2, 4 * g:4 * g + n, (j % 2) * P:(j % 2 + 1) * P],
                             bank(ring_bank((j, g)), 0, n * P).rearrange("p (t q) -> p t q", q=P)
                             ).then_inc(ring_hi, 1)

                def v_to_hi(s):
                    for item in v_items(s):
                        if item[0] == "VT":
                            b = item[1]
                            act.wait_ge(ring_filled, filled(h, item))
                            act.copy(v_hi[:, b * BANK:(b + 1) * BANK], bank(ring_bank(item))
                                     ).then_inc(ring_hi, 1)

                def exponential(j, e):
                    b, end = exps_of(j)[e]
                    n = min(end * BANK, (j + 1) * P) - b * BANK
                    at = score_bank(j, b) * BANK
                    if e == 0:
                        act.wait_ge(negmaxed, TILES * h + j + 1)
                    act.activation(probs[:, j % 2, b * BANK:b * BANK + n], ps[:, at:at + n], ACT.Exp,
                                   bias=neg_max[:, j:j + 1], accum_out=row_part[:, j, e:e + 1]
                                   ).then_inc(exped, 1)

                def z_to_hi(c):
                    act.wait_ge(z_product, CHUNKS * h + c + 1)
                    act.copy(z_hi[:, :], bank(Z, 0, CHUNK_Q)).then_inc(z_hi_done, 1)

                def output(c):
                    act.wait_ge(rcp_done, CHUNKS * h + c + 1)
                    act.wait_ge(out_added, CHUNKS * h + c - 1 + SHARE_FREE)
                    act.wait_ge(wo_product, CHUNKS * h + c + 1)
                    for t in range(2):
                        j = 2 * c + t
                        ins = act.activation(share[:, c % 2, t, :],
                                             bank(ring_bank(("O", c)), t * D, (t + 1) * D), ACT.Copy,
                                             scale=row_rcp[:, j:j + 1])
                    ins.then_inc(shared, 1)

                for s in range(TILES):
                    nt = banks_of(s - 1) if s else 0
                    z = s >= 5 and s % 2
                    if z:
                        z_to_hi((s - 5) // 2)
                    if s == 5:
                        v_to_hi(4)
                    if nt:
                        p_to_hi(s - 1, 0)
                    for g in range(1, min(nt, 3)):
                        p_to_hi(s - 1, g)
                    exponential(s, 0)
                    if nt == 4:
                        p_to_hi(s - 1, 3)
                    if len(exps_of(s)) == 2:
                        exponential(s, 1)
                    if z:
                        output((s - 5) // 2)
                    if s != 4:
                        v_to_hi(s)
                z_to_hi(CHUNKS - 2)
                p_to_hi(TILES - 1, 0)
                p_to_hi(TILES - 1, 1)
                if not last:
                    project(h + 1, 0, 2)
                output(CHUNKS - 2)
                p_to_hi(TILES - 1, 2)
                if not last:
                    project(h + 1, 2, QUARTERS - 1)
                p_to_hi(TILES - 1, 3)
                if not last:
                    project(h + 1, QUARTERS - 1, QUARTERS)
                z_to_hi(CHUNKS - 1)
                if not last:
                    project(h + 1, QUARTERS, PROJ)
                output(CHUNKS - 1)

            act.activation(table_use[:, 2:3], ones[:, :], ACT.Exp)
            project(0, 0, PROJ)
            with act.Fori(0, HEADS - 1) as h:
                head(h, False)
            head(HEADS - 1, True)

        @block.vector
        def _(dve):
            def normalize(p):
                dve.wait_ge(rstd_done, p // 2 + 1)
                if p >= 2:
                    dve.wait_ge(xn_transposed, p - 1)
                for i in (2 * p, 2 * p + 1):
                    dve.tensor_scalar(xn[:, i % 4, :], acc[:, i, :], mean_var[:, i, 0:1], rstd[:, i:i + 1],
                                      ALU.subtract, ALU.mult).then_inc(xn_done, 1)

            def xt_to_lo(p):
                dve.wait_ge(xt_hi_done, p + 1)
                sl = slice(p * 2 * P, (p + 1) * 2 * P)
                dve.tensor_tensor(xt_lo[:, :, sl], bank(TRANS + p % 4).rearrange("p (k q) -> p k q", k=KD),
                                  xt_hi[:, :, sl].bitcast(F32), ALU.subtract).then_inc(xt_lo_done, 1)

            def variances(c):
                q = slice(c * PER_Q, (c + 1) * PER_Q)
                dve.wait_ge(x_loaded[c], 16)
                for t in range(PER_Q):
                    dve.bn_stats(stats[:, t, :], acc[:, c * PER_Q + t, :]).then_inc(stats_done, 1)
                dve.wait_ge(stats_done, PER_Q * (c + 1))
                for t in range(PER_Q):
                    dve.bn_aggr(mean_var[:, c * PER_Q + t, :], stats[:, t, :]).then_inc(aggr_done, 1)
                dve.wait_ge(aggr_done, PER_Q * (c + 1))
                dve.tensor_scalar(inv_var[:, q], mean_var[:, q, 1], EPS, None, ALU.add).then_inc(eps_done, 1)
                dve.wait_ge(eps_done, c + 1)
                dve.reciprocal(inv_var[:, q], inv_var[:, q]).then_inc(inv_done, 1)

            def multiply(c, t):
                dve.wait_ge(up_product, HT * c + t + 1)
                dve.wait_ge(gate_done, HT * c + t + 1)
                dve.wait_ge(hid_lo_done, HT * c + t - 1 + G_FREE)
                dve.tensor_tensor(hidden[t % 2], gate[t % 2], bank(2 * (t % 2) + 1), ALU.mult
                                  ).then_inc(hidden_done, 1)

            def hidden_to_lo(c, t):
                sl = slice((t % 4) * BANK, (t % 4 + 1) * BANK)
                dve.wait_ge(hid_hi_done, HT * c + t + 1)
                dve.tensor_tensor(hid_lo[:, sl], hidden[t % 2], hid_hi[:, sl].bitcast(F32),
                                  ALU.subtract).then_inc(hid_lo_done, 1)

            def add_ffn(c):
                for t in range(PER_Q):
                    a = acc[:, bass.ds(c * PER_Q + t, 1), :].rearrange("p a d -> p (a d)")
                    dve.wait_ge(ffn_product, PER_Q * c + t + 1)
                    dve.tensor_tensor(a, bank(TRANS + t, 0, D), a, ALU.add).then_inc(ffn_added, 1)

            variances(0)
            normalize(0)
            normalize(1)
            xt_to_lo(0)
            xt_to_lo(1)
            variances(1)
            dve.wait_ge(w13_hi_done, 1)
            dve.tensor_tensor(w1_lo, w1_raw, w1_hi.bitcast(F32), ALU.subtract).then_inc(w13_lo_done, 1)
            dve.wait_ge(w13_hi_done, 2)
            dve.tensor_tensor(w3_lo, w3_raw, w3_hi.bitcast(F32), ALU.subtract).then_inc(w13_lo_done, 1)
            dve.wait_ge(had_copied, 2)
            dve.memset(bank_max[:, 1, :], 0.0).then_inc(hidden_done, G_FREE)
            dve.memset(bank_max[:, 2, :], 0.0).then_inc(hid_lo_done, G_FREE)
            variances(2)
            variances(3)
            normalize(2)
            normalize(3)

            for t in range(HT):
                multiply(0, t)
                for p in PAIRS_AFTER[t]:
                    xt_to_lo(p)
                    if p + 2 < TILES // 2:
                        normalize(p + 2)
                if t >= 1:
                    hidden_to_lo(0, t - 1)
                if t == 2:
                    dve.memset(bank_max[:, 0, :], 0.0).then_inc(ffn_added, 1)
            hidden_to_lo(0, HT - 1)
            add_ffn(0)

            with dve.Fori(1, QUARTERS) as c:
                for t in range(HT):
                    multiply(c, t)
                    if t >= 1:
                        hidden_to_lo(c, t - 1)
                hidden_to_lo(c, HT - 1)
                add_ffn(c)

            dve.wait_ge(ffn_added, PER_Q * QUARTERS + 1)
            dve.memset(bank_max[:, 0, :], 0.0).then_inc(ring_freed, R_FREE)
            dve.memset(bank_max[:, 1, :], 0.0).then_inc(z_lo_done, Z_FREE)
            dve.memset(bank_max[:, 2, :], 0.0).then_inc(shared, O_FREE)

            def project(hh, first, last):
                for i in range(first, last):
                    b = i % QUARTERS
                    hi, lo = ((k_hi, k_lo), (q_hi, q_lo))[i // QUARTERS]
                    sl = slice(b * BANK, (b + 1) * BANK)
                    dve.wait_ge(proj_hi, PROJ * hh + i + 1)
                    if i < QUARTERS:
                        dve.tensor_tensor(lo[:, sl], bank(b), hi[:, sl].bitcast(F32),
                                          ALU.subtract).then_inc(proj_lo, 1)
                    else:
                        dve.scalar_tensor_tensor(out=lo[:, sl], in0=bank(b), scalar=SCALE,
                                                 in1=hi[:, sl].bitcast(F32), op0=ALU.mult,
                                                 op1=ALU.subtract).then_inc(proj_lo, 1)

            def head(h, last):
                def maximum(j, b):
                    n = min(BANK, (j + 1) * P - b * BANK)
                    at = score_bank(j, b) * BANK
                    dve.wait_ge(scored, HEAD_BANKS * h + TB[j] + b + 1)
                    if b == banks_of(j) - 1:
                        dve.memset(wait_mark[:, :], 0.0)
                        dve.tensor_tensor_reduce(
                            out=ps[:, at:at + n], in0=ps[:, at:at + n], in1=mask[:, BANK - n:], scale=1.0,
                            scalar=-3e38, op0=ALU.add, op1=ALU.max, accum_out=bank_max[:, j, b:b + 1]
                        ).then_inc(maxed, 1)
                    else:
                        dve.tensor_reduce(bank_max[:, j, b:b + 1], ps[:, at:at + n], AX_X, ALU.max
                                          ).then_inc(maxed, 1)

                def negated_maximum(j):
                    dve.wait_ge(maxed, TB[TILES] * h + TB[j + 1])
                    dve.tensor_reduce(neg_max[:, j:j + 1], bank_max[:, j, 0:banks_of(j)], AX_X, ALU.max,
                                      negate=True).then_inc(negmaxed, 1)

                def p_to_lo(j, g):
                    n = min(4, j + 1 - 4 * g)
                    dve.wait_ge(ring_hi, split_hi(h, (j, g)))
                    where = (slice(None), (j // 2) % 2, slice(4 * g, 4 * g + n),
                             slice((j % 2) * P, (j % 2 + 1) * P))
                    dve.tensor_tensor(pt_lo4[where],
                                      bank(ring_bank((j, g)), 0, n * P).rearrange("p (t q) -> p t q", q=P),
                                      pt_hi4[where].bitcast(F32), ALU.subtract).then_inc(ring_freed, 1)

                def v_out(s):
                    for item in v_items(s):
                        b = item[1]
                        sl = slice(b * BANK, (b + 1) * BANK)
                        if item[0] == "V":
                            dve.wait_ge(ring_filled, filled(h, item))
                            dve.tensor_copy(v_raw[b % 2], bank(ring_bank(item))).then_inc(ring_freed, 1)
                        else:
                            dve.wait_ge(ring_hi, split_hi(h, item))
                            dve.tensor_tensor(v_lo[:, sl], bank(ring_bank(item)), v_hi[:, sl].bitcast(F32),
                                              ALU.subtract).then_inc(ring_freed, 1)

                def z_to_lo(c):
                    dve.wait_ge(z_hi_done, CHUNKS * h + c + 1)
                    dve.tensor_tensor(z_lo[:, :], bank(Z, 0, CHUNK_Q), z_hi[:, :].bitcast(F32),
                                      ALU.subtract).then_inc(z_lo_done, 1)

                def reciprocals(c):
                    j = 2 * c
                    dve.wait_ge(exped, EX[TILES] * h + EX[j + 2])
                    if len(exps_of(j)) == 1:
                        dve.reciprocal(row_rcp[:, j:j + 2], row_part[:, j:j + 2, 0]).then_inc(rcp_done, 1)
                    else:
                        dve.tensor_tensor(row_sum[:, j:j + 2], row_part[:, j:j + 2, 0], row_part[:, j:j + 2, 1],
                                          ALU.add).then_inc(summed, 1)
                        dve.wait_ge(summed, (CHUNKS // 2) * h + c - CHUNKS // 2 + 1)
                        dve.reciprocal(row_rcp[:, j:j + 2], row_sum[:, j:j + 2]).then_inc(rcp_done, 1)

                for s in range(TILES):
                    nt, nb = banks_of(s - 1) if s else 0, banks_of(s)
                    early = 1 if nb > 2 and not ORDERS[s].startswith("sss") else 0
                    maximum(s, 0)
                    if s >= 5 and s % 2:
                        z_to_lo((s - 5) // 2)
                        reciprocals((s - 5) // 2)
                    if s == 5:
                        v_out(4)
                    if nb > 1:
                        maximum(s, 1)
                    for g in range(early):
                        p_to_lo(s - 1, g)
                    for b in range(2, nb):
                        maximum(s, b)
                    negated_maximum(s)
                    for g in range(early, nt):
                        p_to_lo(s - 1, g)
                    if s != 4:
                        v_out(s)
                z_to_lo(CHUNKS - 2)
                p_to_lo(TILES - 1, 0)
                p_to_lo(TILES - 1, 1)
                reciprocals(CHUNKS - 2)
                reciprocals(CHUNKS - 1)
                if not last:
                    project(h + 1, 0, 2)
                p_to_lo(TILES - 1, 2)
                if not last:
                    project(h + 1, 2, QUARTERS - 1)
                p_to_lo(TILES - 1, 3)
                if not last:
                    project(h + 1, QUARTERS - 1, QUARTERS)
                z_to_lo(CHUNKS - 1)
                if not last:
                    project(h + 1, QUARTERS, PROJ)

            dve.wait_ge(mask_ready, 2)
            project(0, 0, PROJ)
            with dve.Fori(0, HEADS - 1) as h:
                head(h, False)
            head(HEADS - 1, True)

        @block.tensor
        def _(pe):
            def mm3(dst, a, b, start, stop):
                pe.matmul(dst, a[0], b[0], start=start, stop=False, skip_group_check=True)
                pe.matmul(dst, a[0], b[1], start=False, stop=False, skip_group_check=True)
                return pe.matmul(dst, a[1], b[0], start=False, stop=stop, skip_group_check=True)

            def transpose_xn(p):
                pe.wait_ge(xn_done, 2 * p + 2)
                if p >= 4:
                    pe.wait_ge(xt_lo_done, p - 3)
                for k in range(KD):
                    for t in range(2):
                        i = 2 * p + t
                        ins = pe.transpose(bank(TRANS + p % 4, (2 * k + t) * P, (2 * k + t + 1) * P),
                                           xn[:, i % 4, k * P:(k + 1) * P], ident[:, :])
                ins.then_inc(xn_transposed, 1)

            def gate_and_up(c, t):
                pe.wait_ge(hidden_done, HT * c + t - 1 + G_FREE)
                for b, hi, lo, done in ((0, w1_hi, w1_lo, gate_product), (1, w3_hi, w3_lo, up_product)):
                    for k in range(KD):
                        sl = slice(k * HID + t * P, k * HID + (t + 1) * P)
                        xs = (xt_hi[:, k, bass.ds(c * BANK, BANK)], xt_lo[:, k, bass.ds(c * BANK, BANK)])
                        ins = mm3(bank(2 * (t % 2) + b), (hi[:, sl], lo[:, sl]), xs, k == 0, k == KD - 1)
                    ins.then_inc(done, 1)

            def down(c, t):
                pe.wait_ge(hid_lo_done, HT * c + t + 1 + G_FREE)
                if t == 0:
                    pe.wait_ge(w2_lo_done, 1)
                    pe.wait_ge(ffn_added, PER_Q * c + 1)
                for q in range(PER_Q):
                    sl = slice((t % 4) * BANK + q * P, (t % 4) * BANK + (q + 1) * P)
                    ins = mm3(bank(TRANS + q, 0, D), (hid_hi[:, sl], hid_lo[:, sl]),
                              (w2_hi[:, t * D:(t + 1) * D], w2_lo[:, t * D:(t + 1) * D]), t == 0, t == HT - 1)
                    if t == HT - 1:
                        ins.then_inc(ffn_product, 1)

            pe.wait_ge(const_ready, 3)
            transpose_xn(0)
            transpose_xn(1)

            pe.wait_ge(had_loaded, 16)
            pe.wait_ge(w2_loaded, 16)
            for i in range(4):
                pe.matmul(bank(i), had, w2_a[:, i * BANK:(i + 1) * BANK], start=True, stop=True
                          ).then_inc(had_product, 1)

            pe.wait_ge(xt_lo_done, 2)
            pe.wait_ge(w13_lo_done, 2)
            for t in range(4):
                gate_and_up(0, t)
                for p in PAIRS_AFTER[t]:
                    transpose_xn(p)
            for t in range(HT):
                down(0, t)
                if t + 4 < HT:
                    gate_and_up(0, t + 4)

            with pe.Fori(1, QUARTERS) as c:
                for t in range(HT):
                    gate_and_up(c, t)
                    if t >= 2:
                        down(c, t - 2)
                down(c, HT - 2)
                down(c, HT - 1)

            def project_slice(dst, w, sl):
                for k in range(KD):
                    ws = slice(k * P, (k + 1) * P)
                    ins = mm3(dst, (wqkv_hi[:, w, ws], wqkv_lo[:, w, ws]),
                              (xt_hi[:, k, sl], xt_lo[:, k, sl]), k == 0, k == KD - 1)
                return ins

            def project(hh, first, last):
                for i in range(first, last):
                    b = i % QUARTERS
                    if i >= QUARTERS:
                        pe.wait_ge(proj_lo, PROJ * hh + i - QUARTERS + 1)
                    project_slice(bank(b), 1 - i // QUARTERS, slice(b * BANK, (b + 1) * BANK)
                                  ).then_inc(projected, 1)

            def head(h, last):
                def scores(j, b):
                    if j < 4:
                        pe.wait_ge(proj_lo, PROJ * h + QUARTERS + j + 1)
                    elif b == 0 or exp_of(*BANK_OF[TB[j] + b - 4]) != exp_of(*BANK_OF[TB[j] + b - 5]):
                        pe.wait_ge(exped, EX[TILES] * h + exp_of(*BANK_OF[TB[j] + b - 4]) + 1)
                    n = min(BANK, (j + 1) * P - b * BANK)
                    qs, ks = slice(j * P, (j + 1) * P), slice(b * BANK, b * BANK + n)
                    dst = bank(score_bank(j, b), 0, n)
                    mm3(dst, (q_hi[:, qs], q_lo[:, qs]), (k_hi[:, ks], k_lo[:, ks]), True, True
                        ).then_inc(scored, 1)

                def ring_wait(item):
                    n = ITEM[item] - RING
                    hh, before = (h, ITEMS[n]) if n >= 0 else (h - 1, ITEMS[n] or ITEMS[n - RING])
                    if before[0] == "O":
                        pe.wait_ge(shared, CHUNKS * hh + before[1] + 1 + O_FREE)
                    else:
                        pe.wait_ge(ring_freed, freed(hh, before))

                def transposes(j, g):
                    if g == 0 or exp_of(j, g) != exp_of(j, g - 1):
                        pe.wait_ge(exped, EX[TILES] * h + exp_of(j, g) + 1)
                    ring_wait((j, g))
                    for i in range(4 * g, min(4 * g + 4, j + 1)):
                        ins = pe.transpose(bank(ring_bank((j, g)), (i % 4) * P, (i % 4 + 1) * P),
                                           probs[:, j % 2, i * P:(i + 1) * P], ident[:, :])
                    ins.then_inc(ring_filled, 1)

                def v(s):
                    for item in v_items(s):
                        what, b = item
                        ring_wait(item)
                        if what == "V":
                            project_slice(bank(ring_bank(item)), 2, slice(b * BANK, (b + 1) * BANK)
                                          ).then_inc(ring_filled, 1)
                        else:
                            pe.wait_ge(ring_freed, freed(h, ("V", b)))
                            for t in range(PER_Q):
                                ins = pe.transpose(bank(ring_bank(item), t * P, (t + 1) * P),
                                                   v_raw[b % 2][:, t * P:(t + 1) * P], ident[:, :])
                            ins.then_inc(ring_filled, 1)

                def weighted_sum(c, first, last):
                    if first == 0:
                        pe.wait_ge(z_lo_done, CHUNKS * h + c + Z_FREE)
                    for i in range(first, last):
                        if i % 4 == 0 or i == first:
                            pe.wait_ge(ring_freed, freed(h, (2 * c + 1, i // 4)))
                        lo = P if i == 2 * c + 1 else 0
                        ks = slice(i * P, (i + 1) * P)
                        ins = mm3(bank(Z, lo, CHUNK_Q), (v_hi[:, ks], v_lo[:, ks]),
                                  (pt_hi4[:, c % 2, i, lo:CHUNK_Q], pt_lo4[:, c % 2, i, lo:CHUNK_Q]),
                                  i == 0, i == 2 * c + 1)
                    if last == 2 * c + 2:
                        ins.then_inc(z_product, 1)

                def output(c):
                    pe.wait_ge(z_lo_done, CHUNKS * h + c + 1 + Z_FREE)
                    ring_wait(("O", c))
                    if c == 0:
                        pe.wait_ge(wo_split, h + 1)
                    for t in range(2):
                        qs = slice(t * P, (t + 1) * P)
                        ins = mm3(bank(ring_bank(("O", c)), t * D, (t + 1) * D), (z_hi[:, qs], z_lo[:, qs]),
                                  (wo_hi[:, :], wo_lo[:, :]), True, True)
                    ins.then_inc(wo_product, 1)

                for s in range(TILES):
                    nt = banks_of(s - 1) if s else 0
                    for n, what in enumerate(ORDERS[s]):
                        b = ORDERS[s][:n].count(what)
                        if what == "s":
                            scores(s, b)
                        else:
                            transposes(s - 1, b)
                    v(s)
                    part = []
                    if s >= 3 and s % 2:
                        c = (s - 3) // 2
                        part = [(c, 0, (c + 1) // 2), (c, (c + 1) // 2, c + 1)]
                    elif s >= 4:
                        c = (s - 4) // 2
                        part = [(c, c + 1, c + 1 + (c + 1) // 2), (c, c + 1 + (c + 1) // 2, 2 * c + 2)]
                    for n, (c, a, b) in enumerate(part):
                        if a < b:
                            weighted_sum(c, a, b)
                        if n == 0 and nt == 4:
                            transposes(s - 1, 3)
                        if n == 1 and s >= 5 and s % 2:
                            output((s - 5) // 2)
                c = CHUNKS - 1
                weighted_sum(c - 1, c, 2 * c)
                transposes(TILES - 1, 0)
                transposes(TILES - 1, 1)
                if not last:
                    pe.wait_ge(wqkv_split, h + 2)
                    pe.wait_ge(exped, EX[TILES] * h + EX[TILES])
                    project(h + 1, 0, 1)
                if not last:
                    project(h + 1, 1, 2)
                output(c - 1)
                transposes(TILES - 1, 2)
                if not last:
                    project(h + 1, 2, QUARTERS - 1)
                transposes(TILES - 1, 3)
                if not last:
                    project(h + 1, QUARTERS - 1, QUARTERS)
                weighted_sum(c, 0, c + 1)
                weighted_sum(c, c + 1, 2 * c + 2)
                if not last:
                    project(h + 1, QUARTERS, PROJ)
                output(c)

            pe.wait_ge(wqkv_split, 1)
            pe.wait_ge(hidden_done, HT * QUARTERS + G_FREE)
            project(0, 0, PROJ)
            with pe.Fori(0, HEADS - 1) as h:
                head(h, False)
            head(HEADS - 1, True)


def kernel(L0_attn_x, L0_attn_W_K, L0_attn_W_Q, L0_attn_W_V, L0_attn_W_O, L0_ffn_W1, L0_ffn_W2, L0_ffn_W3):
    import numpy as np
    import concourse.bacc as bacc
    from concourse.bass_utils import run_bass_kernel_spmd

    x = np.ascontiguousarray(L0_attn_x)[0]
    heads, dh, d = L0_attn_W_Q.shape
    hid = L0_ffn_W1.shape[0]

    def by_model(w):
        return np.asarray(w).T.reshape(d // P, P, -1).transpose(1, 0, 2)

    def head_weights(w):
        return np.asarray(w).transpose(0, 2, 1).reshape(heads, d // P, P, dh).transpose(0, 2, 1, 3).reshape(
            heads, P, -1)

    w_o = np.asarray(L0_attn_W_O).T.reshape(heads, dh, d)
    h128 = np.array([[1 - 2 * (bin(i & j).count("1") & 1) for j in range(P)] for i in range(P)], np.float32)
    arrays = {
        "x": x,
        "w_heads": np.ascontiguousarray(np.stack(
            [head_weights(L0_attn_W_Q), head_weights(L0_attn_W_K), head_weights(L0_attn_W_V), w_o], axis=2)),
        "w1t": np.ascontiguousarray(by_model(L0_ffn_W1)),
        "w3t": np.ascontiguousarray(by_model(L0_ffn_W3)),
        "w2t": np.ascontiguousarray(np.asarray(L0_ffn_W2).T.reshape(hid // P, P, d).transpose(1, 0, 2)),
        "hadamard": h128,
    }
    nc = bacc.Bacc("TRN2", target_bir_lowering=False, num_devices=1)
    args = [nc.dram_tensor(n, a.shape, mybir.dt.from_np(a.dtype), kind="ExternalInput").ap()
            for n, a in arrays.items()]
    out = nc.dram_tensor("out", x.shape, F32, kind="ExternalOutput").ap()
    attention_ffn_kernel(nc, *args, out)
    r = run_bass_kernel_spmd(nc, [arrays], core_ids=[0])
    return r.results[0]["out"].reshape(L0_attn_x.shape)
```
